# Optimizing a Trainium2 kernel written in Bass

```python
import numpy as np
import jax
import jax.numpy as jnp

def _softmax(x, axis=-1):
    return jax.nn.softmax(x, axis=axis)

def _gelu(x):
    return jax.nn.gelu(x, approximate=True)

def _silu(x):
    return jax.nn.silu(x)

def _sigmoid(x):
    return jax.nn.sigmoid(x)

def _layernorm(x, axis=-1, eps=1e-05):
    m = jnp.mean(x, axis=axis, keepdims=True)
    v = jnp.var(x, axis=axis, keepdims=True)
    return (x - m) / jnp.sqrt(v + eps)

def _scatter_add(tgt, idx, src, axis=0):
    return tgt.at[idx].add(src)

def _segment_sum(src, seg, n):
    return jax.ops.segment_sum(src, seg, n)
kernel_name = 'mk_audio_tower_d1_tok_audfeat256_r4_9af0e5'

def setup_inputs(seed: int=0):
    np.random.seed(seed)
    _w = jnp.asarray

    def _rec_inputs():
        import jax
        import jax.numpy as jnp
        _rk = jax.random.key(seed)
        x = -5.07413e-05 + 0.999912 * jax.random.normal(jax.random.fold_in(_rk, 1), (128, 125, 64), jnp.float32)
        return x
    x = _rec_inputs()

    def _L0_tok_setup():
        import jax, jax.numpy as jnp
        from jax import lax
        import numpy as np
        B, T, C, K, STRIDE = (16, 4000, 64, 5, 2)
        EPS = 0.001
        key = jax.random.key(seed)
        k0, k1, k2, k3 = jax.random.split(key, 4)
        x = jax.random.normal(k0, (B, T, C), dtype=jnp.float32)
        w = jax.random.normal(k1, (K, 1, C), dtype=jnp.float32) * 0.1
        b = jax.random.normal(k2, (C,), dtype=jnp.float32) * 0.01
        gamma = jnp.ones((C,), dtype=jnp.float32)
        beta = jnp.zeros((C,), dtype=jnp.float32)
        alpha = jnp.full((C,), 0.25, dtype=jnp.float32) + 0.01 * jax.random.normal(k3, (C,), dtype=jnp.float32)
        return {'x': x, 'w': w, 'b': b, 'gamma': gamma, 'beta': beta, 'alpha': alpha}
    _L0_tok_all = _L0_tok_setup()
    _L0_tok_in = {k: v for k, v in _L0_tok_all.items() if k in ('w', 'b', 'gamma', 'beta', 'alpha')}
    del _L0_tok_all

    def _L0_attn_setup():
        import jax, jax.numpy as jnp
        import numpy as np

        def phi_1(z):
            eps = 1e-12
            mask = jnp.abs(z) < eps
            z_safe = jnp.where(mask, eps, z)
            return jnp.where(mask, 1.0, jnp.expm1(z_safe) / z_safe)
        key = jax.random.key(seed)
        ks = jax.random.split(key, 4)
        B, L, Dm, N = (4, 512, 64, 16)
        u = jax.random.normal(ks[0], (B, L, Dm), dtype=jnp.float32)
        A_log = jnp.log(jnp.arange(1, N + 1, dtype=jnp.float32) * 0.1)
        D_param = jnp.ones((Dm,), jnp.float32)
        scale = jnp.ones((Dm,), jnp.float32)
        W_dt = jax.random.normal(ks[1], (Dm, Dm), dtype=jnp.float32) * 0.02
        b_dt = jnp.zeros((Dm,), jnp.float32)
        W_B = jax.random.normal(ks[2], (N, Dm), dtype=jnp.float32) * 0.02
        b_B = jnp.zeros((N,), jnp.float32)
        W_C = jax.random.normal(ks[3], (N, Dm), dtype=jnp.float32) * 0.02
        b_C = jnp.zeros((N,), jnp.float32)
        return dict(u=u, A_log=A_log, D_param=D_param, scale=scale, W_dt=W_dt, b_dt=b_dt, W_B=W_B, b_B=b_B, W_C=W_C, b_C=b_C)
    _L0_attn_all = _L0_attn_setup()
    _L0_attn_in = {k: v for k, v in _L0_attn_all.items() if k in ('A_log', 'D_param', 'scale', 'W_dt', 'b_dt', 'W_B', 'b_B', 'W_C', 'b_C')}
    del _L0_attn_all

    def _L0_ffn_setup():
        import jax, jax.numpy as jnp
        import numpy as np
        D_IN, D_HID, D_OUT = (64, 128, 64)
        N_EXPERTS, TOP_K = (64, 2)
        B, S = (8, 1024)
        key = jax.random.key(seed)
        ks = jax.random.split(key, 8)
        scale_in = 1.0 / np.sqrt(D_IN)
        scale_hid = 1.0 / np.sqrt(D_HID)
        return {'x': jax.random.normal(ks[0], (B, S, D_IN), dtype=jnp.float32), 'Wr': jax.random.uniform(ks[1], (D_IN, N_EXPERTS), jnp.float32, -scale_in, scale_in), 'br': jax.random.uniform(ks[2], (N_EXPERTS,), jnp.float32, -scale_in, scale_in), 'W1': jax.random.uniform(ks[3], (N_EXPERTS, D_IN, D_HID), jnp.float32, -scale_in, scale_in), 'b1': jax.random.uniform(ks[4], (N_EXPERTS, D_HID), jnp.float32, -scale_in, scale_in), 'W2': jax.random.uniform(ks[5], (N_EXPERTS, D_HID, D_OUT), jnp.float32, -scale_hid, scale_hid), 'b2': jax.random.uniform(ks[6], (N_EXPERTS, D_OUT), jnp.float32, -scale_hid, scale_hid)}
    _L0_ffn_all = _L0_ffn_setup()
    _L0_ffn_in = {k: v for k, v in _L0_ffn_all.items() if k in ('Wr', 'br', 'W1', 'b1', 'W2', 'b2')}
    del _L0_ffn_all
    return {'x': x, 'L0_tok_w': _L0_tok_in['w'], 'L0_tok_b': _L0_tok_in['b'], 'L0_tok_gamma': _L0_tok_in['gamma'], 'L0_tok_beta': _L0_tok_in['beta'], 'L0_tok_alpha': _L0_tok_in['alpha'], 'L0_attn_A_log': _L0_attn_in['A_log'], 'L0_attn_D_param': _L0_attn_in['D_param'], 'L0_attn_scale': _L0_attn_in['scale'], 'L0_attn_W_dt': _L0_attn_in['W_dt'], 'L0_attn_b_dt': _L0_attn_in['b_dt'], 'L0_attn_W_B': _L0_attn_in['W_B'], 'L0_attn_b_B': _L0_attn_in['b_B'], 'L0_attn_W_C': _L0_attn_in['W_C'], 'L0_attn_b_C': _L0_attn_in['b_C'], 'L0_ffn_Wr': _L0_ffn_in['Wr'], 'L0_ffn_br': _L0_ffn_in['br'], 'L0_ffn_W1': _L0_ffn_in['W1'], 'L0_ffn_b1': _L0_ffn_in['b1'], 'L0_ffn_W2': _L0_ffn_in['W2'], 'L0_ffn_b2': _L0_ffn_in['b2']}

def reference(x, L0_tok_w, L0_tok_b, L0_tok_gamma, L0_tok_beta, L0_tok_alpha, L0_attn_A_log, L0_attn_D_param, L0_attn_scale, L0_attn_W_dt, L0_attn_b_dt, L0_attn_W_B, L0_attn_b_B, L0_attn_W_C, L0_attn_b_C, L0_ffn_Wr, L0_ffn_br, L0_ffn_W1, L0_ffn_b1, L0_ffn_W2, L0_ffn_b2):
    import jax
    import jax.numpy as jnp

    def _L0_tok_ref(x, w, b, gamma, beta, alpha):
        import jax, jax.numpy as jnp
        from jax import lax
        import numpy as np
        B, T, C, K, STRIDE = (16, 4000, 64, 5, 2)
        EPS = 0.001
        y = lax.conv_general_dilated(x, w, window_strides=(STRIDE,), padding='SAME', dimension_numbers=('NWC', 'WIO', 'NWC'), feature_group_count=C) + b
        mean = jnp.mean(y, axis=(1, 2), keepdims=True)
        var = jnp.var(y, axis=(1, 2), keepdims=True)
        yn = (y - mean) * lax.rsqrt(var + EPS) * gamma + beta
        return jnp.where(yn > 0, yn, alpha * yn)

    def _L0_attn_ref(u, A_log, D_param, scale, W_dt, b_dt, W_B, b_B, W_C, b_C):
        import jax, jax.numpy as jnp
        import numpy as np

        def phi_1(z):
            eps = 1e-12
            mask = jnp.abs(z) < eps
            z_safe = jnp.where(mask, eps, z)
            return jnp.where(mask, 1.0, jnp.expm1(z_safe) / z_safe)
        B, L, Dm = u.shape
        N = A_log.shape[0]
        dt_input = u @ W_dt.T + b_dt
        B_vec = u @ W_B.T + b_B
        C_vec = u @ W_C.T + b_C
        dt = jax.nn.softplus(dt_input)
        A = -jnp.exp(A_log)
        dtA = dt[..., None] * A
        dA = jnp.exp(dtA)
        b = phi_1(dtA) * B_vec[:, :, None, :] * u[..., None]
        a_t = jnp.moveaxis(dA, 1, 0)
        b_t = jnp.moveaxis(b, 1, 0)
        h0 = jnp.zeros((B, Dm, N), u.dtype)

        def step(h, ab):
            a, bb = ab
            h = a * h + bb
            return (h, h)
        _, h_traj = jax.lax.scan(step, h0, (a_t, b_t))
        h_traj = jnp.moveaxis(h_traj, 0, 1)
        h_contrib = jnp.einsum('bln,bldn->bld', C_vec, h_traj)
        y_raw = h_contrib + D_param * u
        return y_raw * scale

    def _L0_ffn_ref(x, Wr, br, W1, b1, W2, b2):
        import jax, jax.numpy as jnp
        import numpy as np
        D_IN, D_HID, D_OUT = (64, 128, 64)
        N_EXPERTS, TOP_K = (64, 2)
        B, S = (8, 1024)
        Bx, Sx, D = x.shape
        xf = x.reshape(-1, D)
        T = xf.shape[0]
        E = Wr.shape[1]
        logits = xf @ Wr + br
        topk_logits, topk_idx = jax.lax.top_k(logits, TOP_K)
        gates = jax.nn.softmax(topk_logits, axis=1)
        combine = jnp.zeros((T, E), xf.dtype).at[jnp.arange(T)[:, None], topk_idx].add(gates)
        out = jnp.zeros((T, W2.shape[-1]), xf.dtype)
        for e in range(E):
            h = jax.nn.relu(xf @ W1[e] + b1[e])
            y = h @ W2[e] + b2[e]
            out = out + combine[:, e:e + 1] * y
        return out.reshape(Bx, Sx, -1)
    h = _L0_tok_ref(x, L0_tok_w, L0_tok_b, L0_tok_gamma, L0_tok_beta, L0_tok_alpha)
    h = h + _L0_attn_ref(_layernorm(h, axis=-1), L0_attn_A_log, L0_attn_D_param, L0_attn_scale, L0_attn_W_dt, L0_attn_b_dt, L0_attn_W_B, L0_attn_b_B, L0_attn_W_C, L0_attn_b_C)
    h = h + _L0_ffn_ref(_layernorm(h, axis=-1), L0_ffn_Wr, L0_ffn_br, L0_ffn_W1, L0_ffn_b1, L0_ffn_W2, L0_ffn_b2)
    return h

_drawn_inputs = setup_inputs


def setup_inputs(seed=0):
    import zlib

    import numpy as np

    out = dict(_drawn_inputs(seed))
    spreads = {'L0_tok_gamma': (1.0, 0.2),
     'L0_tok_beta': (0.0, 0.1),
     'L0_attn_D_param': (1.0, 0.2),
     'L0_attn_scale': (1.0, 0.2),
     'L0_attn_b_dt': (0.0, 0.8),
     'L0_attn_b_B': (0.0, 0.1),
     'L0_attn_b_C': (0.0, 0.1)}
    factors = {'L0_tok_alpha': 2.847, 'L0_attn_W_dt': 7.581, 'L0_ffn_b1': 5.021, 'L0_ffn_b2': 2.835}
    for name, (base, spread) in spreads.items():
        noise = np.random.default_rng([zlib.crc32(name.encode()), seed]).standard_normal(out[name].shape)
        drawn = base * np.exp(spread * noise) if base else spread * noise
        out[name] = jnp.asarray(drawn.astype(out[name].dtype))
    for name, factor in factors.items():
        out[name] = (out[name] * factor).astype(out[name].dtype)
    return out
```

```python
from contextlib import ExitStack

import concourse.bass as bass
from concourse import mybir

F32 = mybir.dt.float32
I32 = mybir.dt.int32
U32 = mybir.dt.uint32
ALU = mybir.AluOpType
ACT = mybir.ActivationFunctionType
AX_X = mybir.AxisListType.X

P = 128
T_IN = 125
C = 64
TAPS = 5
L = 63
GL = 7
NG = L // GL
CHUNKS = 3
GPC = NG // CHUNKS
CL = GL * GPC
N = 16
S = L + 1
DC = 16
NDC = C // DC
U = DC * S
BANK = 512
E = 64
HID = 128
TOK = P * L
PAIRS = 2 * TOK
ROW = 68
TILES = PAIRS // P + E - 1
TPG = 3
GROUPS = TILES // TPG
NOWHERE = 99999.0
EPS_GN = 0.001
EPS_LN = 1e-05
DT_MIN = 1e-19
DT_RESTART = 1e18

NPROJ = C + 2 * N
DVE_HC = (3, 7, 11, 15)
NV = len(DVE_HC)
NPL = N - NV
H_CR, HCV_CR, HCP_CR, ADD_CR, G_CR, H2_CR = 4, 1, 1, 2, 1, 1
ROWS_CR, HID_CR, RTC_CR, YPS_CR = 3, 2, 2, 2


def dve_upto(k):
    return sum(j in DVE_HC for j in range(k + 1)) - sum(j + N in DVE_HC for j in range(k + 1, 0))


def pool_upto(k):
    return k + 1 - dve_upto(k)


class Chain:

    def __init__(self, eng, sem, at=0):
        self.eng, self.sem, self.at = eng, sem, at

    def link(self, ins):
        ins.then_inc(self.sem, 1)
        self.at = self.at + 1
        self.eng.wait_ge(self.sem, self.at)


def build(nc, x, w, b, gamma, beta, alpha, A_log, D_param, scale, W_dt, b_dt, W_B, b_B, W_C, b_C,
          Wr, br, W1, b1, W2, b2, out):
    sorted_rows = nc.dram_tensor("sorted_rows", (TILES * P, ROW), F32, kind="Internal").ap()
    expert_out = nc.dram_tensor("expert_out", (PAIRS, C), F32, kind="Internal").ap()

    with ExitStack() as ctx:
        def sb(name, shape, dt=F32):
            return ctx.enter_context(nc.sbuf_tensor(name, shape, dt))

        def sem(name):
            return ctx.enter_context(nc.semaphore(name))

        XPAIRS = L + 2
        x_w1 = sb("x_w1", [P, XPAIRS * P])
        hg = sb("hg", [P, L, C])
        xp1 = sb("xp1", [P, L, ROW])
        dt_xp2 = sb("dt_xp2", [P, L * ROW])
        xt = sb("xt", [P, XPAIRS * P])
        us_lg = sb("us_lg", [P, C * S])
        bc = sb("bc", [P, 2 * N, S])
        w2s = sb("w2s", [P, E * C])
        w_ring = sb("w_ring", [P, 4, U])
        hh_ring = sb("hh_ring", [P, 5, U])
        ident = sb("ident", [P, P])
        ident2 = sb("ident2", [P, C])
        ones = sb("ones", [P, P])
        tri = sb("tri", [P, P])
        wconv = sb("wconv", [P, 3, C])
        wcol = sb("wcol", [P, 3])
        wst = sb("wst", [NPROJ, C + 1])
        wcat = sb("wcat", [C + 1, NPROJ])
        wr = sb("wr", [C + 1, E])
        vecs = sb("vecs", [P, 6, C])
        a_log = sb("a_log", [P, N])
        a_exp = sb("a_exp", [P, 4, N])
        eps = sb("eps", [P, 3])
        stats = sb("stats", [P, NG, 6])
        gn = sb("gn", [P, 4])
        ln_s = sb("ln_s", [P, 4, CL])
        pad_rows = sb("pad_rows", [P, TPG, ROW])
        mx = sb("mx", [P, L, 8])
        mi = sb("mi", [P, L, 8], U32)
        top = sb("top", [P, 7, L])
        iota_e = sb("iota_e", [P, E])
        iota_e_i = sb("iota_e_i", [P, E], I32)
        small = sb("small", [P, 10, E])
        small_i = sb("small_i", [P, E], I32)
        slot_i = sb("slot_i", [P, 2, L], I32)
        tile_no_i = sb("tile_no_i", [P, 2], I32)
        tile_no = sb("tile_no", [P, 2])
        tile_e = sb("tile_e", [P, 2])
        te = sb("te", [1, 2 * P], I32)
        out_idx = sb("out_idx", [P, 2, TPG], I32)

        uT = xt[0:C + 1, 0:3 * GL * P].rearrange("p (k n) -> p k n", k=3)
        dt = dt_xp2[:, 0:C * S]
        xp2 = dt_xp2[:, :].rearrange("p (l r) -> p l r", r=ROW)
        tmp = xt[:, 0:C * S]
        up = xt[:, C * S:2 * C * S]
        us3 = us_lg[:, :].rearrange("p (d s) -> p d s", s=S)
        logits = us_lg[:, 0:L * E].rearrange("p (l e) -> p l e", e=E)
        mask1 = xt[:, 0:E * L].rearrange("p (e l) -> p e l", l=L)
        mask2 = xt[:, C * S:C * S + E * L].rearrange("p (e l) -> p e l", l=L)
        w_flat = w_ring[:, :, :].rearrange("p k n -> p (k n)")
        b2s = w_flat[0:1, 0:E * C]
        cen = w_flat[:, 0:CL * C].rearrange("p (l d) -> p l d", d=C)
        sq = w_flat[:, CL * C:2 * CL * C].rearrange("p (l d) -> p l d", d=C)
        rank = hh_ring[:, :, :].rearrange("p k n -> p (k n)")[:, 0:E * L]
        rank3 = rank.rearrange("p (e l) -> p e l", l=L)
        w1s = x_w1[0:C + 1, 0:E * HID]
        o = 0
        rows_in = us_lg[:, 0:3 * TPG * ROW].rearrange("p (k t r) -> p k t r", k=3, r=ROW)
        o += 3 * TPG * ROW
        xT_e = us_lg[0:C + 1, o:o + 2 * TPG * P].rearrange("p (k n) -> p k n", k=2)
        o += 2 * TPG * P
        hT_e = us_lg[:, o:o + 2 * TPG * P].rearrange("p (k n) -> p k n", k=2)
        o += 2 * TPG * P
        y_e = us_lg[:, o:o + 2 * TPG * C].rearrange("p (k t d) -> p k t d", k=2, d=C)
        o += 2 * TPG * C
        w1_e = us_lg[0:C + 1, o:o + 2 * TPG * HID].rearrange("p (k t n) -> p k t n", k=2, n=HID)
        y1 = xt[:, 0:L * C].rearrange("p (l d) -> p l d", d=C)
        y2 = xt[:, L * C:2 * L * C].rearrange("p (l d) -> p l d", d=C)

        ps = ctx.enter_context(nc.psum_tensor("ps", [P, 8, BANK], F32))

        def banks(a, n):
            return ps[:, a:a + n, :].rearrange("p k n -> p (k n)")

        s_x = [sem(f"s_x{g}") for g in range(NG)]
        s_settled = sem("s_settled")
        s_xready = sem("s_xready")
        s_vecs = sem("s_vecs")
        s_wcol = sem("s_wcol")
        s_wproj = sem("s_wproj")
        s_moew = sem("s_moew")
        s_b2 = sem("s_b2")
        s_padw = sem("s_padw")
        s_zero = sem("s_zero")
        s_pool = sem("s_pool")
        s_ident = sem("s_ident")
        s_consts = sem("s_consts")
        s_wconv = sem("s_wconv")
        s_xT = sem("s_xT")
        s_xTc = sem("s_xTc")
        s_conv = sem("s_conv")
        s_y = sem("s_y")
        s_wT = sem("s_wT")
        s_wcat = sem("s_wcat")
        s_dve = sem("s_dve")
        s_act = sem("s_act")
        s_gnvar = sem("s_gnvar")
        s_gnsd = sem("s_gnsd")
        s_cen = sem("s_cen")
        s_sq = sem("s_sq")
        s_var = sem("s_var")
        s_sd = sem("s_sd")
        s_ln = sem("s_ln")
        s_uT = sem("s_uT")
        s_uTc = sem("s_uTc")
        s_proj = sem("s_proj")
        s_projc = sem("s_projc")
        s_us = sem("s_us")
        s_aexp = sem("s_aexp")
        s_acols = sem("s_acols")
        s_bdiv = sem("s_bdiv")
        s_lnp = sem("s_lnp")
        s_dt = sem("s_dt")
        s_r0 = sem("s_r0")
        s_up = sem("s_up")
        s_w = sem("s_w")
        s_th = sem("s_th")
        s_dA = sem("s_dA")
        s_g = sem("s_g")
        s_b = sem("s_b")
        s_h = sem("s_h")
        s_hcv = sem("s_hcv")
        s_hcp = sem("s_hcp")
        s_skip = sem("s_skip")
        s_add = sem("s_add")
        s_acc = sem("s_acc")
        s_h2 = sem("s_h2")
        s_lg = sem("s_lg")
        s_lgc = sem("s_lgc")
        s_ediff = sem("s_ediff")
        s_eexp = sem("s_eexp")
        s_gate = sem("s_gate")
        s_xp2 = sem("s_xp2")
        s_msum = sem("s_msum")
        s_cnt = sem("s_cnt")
        s_tot = sem("s_tot")
        s_te = sem("s_te")
        s_teT = sem("s_teT")
        s_tei = sem("s_tei")
        s_slot = sem("s_slot")
        s_disp = sem("s_disp")
        s_rows = [sem(f"s_rows{k}") for k in range(3)]
        s_rT = sem("s_rT")
        s_rTc = sem("s_rTc")
        s_hid = sem("s_hid")
        s_relu = sem("s_relu")
        s_yps = sem("s_yps")
        s_ye = sem("s_ye")
        s_idx = sem("s_idx")
        s_sc = [sem(f"s_sc{k}") for k in range(2)]
        s_yl = [sem(f"s_yl{k}") for k in range(CHUNKS)]
        s_fin = sem("s_fin")
        s_out = sem("s_out")

        def h_buf(k):
            return hh_ring[:, k % 2, :].rearrange("p (d s) -> p d s", s=S)

        def hc_buf(k):
            return hh_ring[:, 2 + k % 2, :].rearrange("p (d s) -> p d s", s=S)

        def settle(eng):
            eng.sem_inc(s_settled, 1)

        block = ctx.enter_context(nc.Block())

        @block.sync
        def _(sp):
            flat = x.rearrange("b t c -> b (t c)")
            cut = [0] + [min((2 * GL * (g + 1) + 2), T_IN) for g in range(NG - 1)] + [T_IN]
            sp.dma_start(wcol[0:C, 0:1], w[4, 0, :].rearrange("(c a) -> c a", a=1)).then_inc(s_wcol, 16)
            for g in range(NG):
                a, z = cut[g] * C, cut[g + 1] * C
                sp.dma_start(x_w1[:, P + a:P + z], flat[:, a:z]).then_inc(s_x[g], 16)
            sp.dma_start(wst[0:C, 0:C], W_dt).then_inc(s_wproj, 16)
            sp.dma_start(wst[C:C + N, 0:C], W_B).then_inc(s_wproj, 16)
            sp.dma_start(wst[C + N:NPROJ, 0:C], W_C).then_inc(s_wproj, 16)
            sp.dma_start(wst[0:C, C:C + 1], b_dt.rearrange("(c a) -> c a", a=1)).then_inc(s_wproj, 16)
            sp.dma_start(wst[C:C + N, C:C + 1], b_B.rearrange("(c a) -> c a", a=1)).then_inc(s_wproj, 16)
            sp.dma_start(wst[C + N:NPROJ, C:C + 1], b_C.rearrange("(c a) -> c a", a=1)).then_inc(s_wproj, 16)
            for g in range(NG):
                sp.wait_ge(s_x[g], 16)
                sp.sem_inc(s_xready, 1)
            sp.wait_ge(s_pool, 7)
            sp.dma_start(sorted_rows.rearrange("(p k t) r -> p k (t r)", p=P, t=TPG),
                         pad_rows[:, :, :].rearrange("p t r -> p (t r)").unsqueeze(1).broadcast_to(
                             [P, GROUPS, TPG * ROW])).then_inc(s_padw, 16)
            sp.dma_start(w2s[:, :].rearrange("k (e d) -> k e d", e=E), W2.rearrange("e k d -> k e d")
                         ).then_inc(s_moew, 16)
            sp.dma_start(wr[0:C, :], Wr).then_inc(s_moew, 16)
            sp.dma_start(wr[C:C + 1, :], br.rearrange("(a e) -> a e", a=1)).then_inc(s_moew, 16)
            sp.wait_ge(s_xT, NG)
            sp.dma_start(w1s[0:C, :].rearrange("k (e h) -> k e h", e=E), W1.rearrange("e k h -> k e h")
                         ).then_inc(s_moew, 16)
            sp.dma_start(w1s[C:C + 1, :], b1.rearrange("(a e) h -> a (e h)", a=1)).then_inc(s_moew, 16)
            sp.wait_ge(s_ln, 2 * CHUNKS)
            sp.dma_start(b2s, b2.rearrange("(a e) d -> a (e d)", a=1)).then_inc(s_b2, 16)
            sp.wait_ge(s_disp, 16 * 2 * L)
            with sp.Fori(0, GROUPS // 3) as q:
                for k in range(3):
                    sp.wait_ge(s_idx, 3 * q + k + 1)
                    sp.wait_ge(s_ye, 3 * q + k + 1)
                    sp.dma_start(rows_in[:, k],
                                 sorted_rows[bass.ds((3 * q + k) * (TPG * P), TPG * P), :].rearrange(
                                     "(t p) r -> p t r", t=TPG)).then_inc(s_rows[k], 16)
            for k in range(2):
                sp.wait_ge(s_sc[k], 16 * TPG * ((GROUPS + 1 - k) // 2))
            eo = expert_out.rearrange("(k b l) d -> k b l d", k=2, l=L)
            for c in range(CHUNKS):
                for k, y in enumerate((y1, y2)):
                    sp.dma_start(y[:, c * CL:(c + 1) * CL, :], eo[k, :, c * CL:(c + 1) * CL, :]
                                 ).then_inc(s_yl[c], 16)
            for c in range(CHUNKS):
                sp.wait_ge(s_fin, c + 1)
                sp.dma_start(out[:, c * CL:(c + 1) * CL, :], hg[:, c * CL:(c + 1) * CL, :]
                             ).then_inc(s_out, 16)
            sp.wait_ge(s_out, 16 * CHUNKS)

        @block.gpsimd
        def _(pool):
            ch = Chain(pool, s_pool)
            ch.link(pool.memset(ident[:, :], 0.0))
            ch.link(pool.memset(ident2[:, :], 0.0))
            pool.affine_select(out=ident[:, :], in_=ident[:, :], compare_op=ALU.not_equal, fill=1.0, base=0,
                               pattern=[[-1, P]], channel_multiplier=1).then_inc(s_ident, 1)
            for s in range(2):
                ch.link(pool.affine_select(out=ident2[:, :], in_=ident2[:, :], compare_op=ALU.not_equal,
                                           fill=1.0, base=-C * s, pattern=[[-1, C]], channel_multiplier=1))
            ch.link(pool.memset(pad_rows[:, :, :], 0.0))
            ch.link(pool.memset(pad_rows[:, :, C:C + 1], 1.0))
            ch.link(pool.memset(pad_rows[:, :, C + 1:C + 2], NOWHERE))
            ch.link(pool.memset(ones[:, :], 1.0))
            ch.link(pool.memset(tri[:, :], 1.0))
            ch.link(pool.affine_select(out=tri[:, :], in_=tri[:, :], compare_op=ALU.is_gt, fill=0.0, base=0,
                                       pattern=[[1, P]], channel_multiplier=-1))
            pool.iota(iota_e_i[:, :], [[1, E]], base=0, channel_multiplier=0).then_inc(s_consts, 1)
            pool.iota(tile_no_i[:, :], [[P, 2]], base=0, channel_multiplier=1).then_inc(s_consts, 1)
            pool.iota(slot_i[:, 0, :], [[1, L]], base=0, channel_multiplier=L).then_inc(s_consts, 1)
            pool.iota(slot_i[:, 1, :], [[1, L]], base=TOK, channel_multiplier=L).then_inc(s_consts, 1)
            pool.memset(us3[:, :, 0:1], 0.0).then_inc(s_consts, 1)
            scale_b = vecs[:, 5, :].unsqueeze(2).broadcast_to([P, C, CL])
            pool.wait_ge(s_vecs, 16 * 6)
            for c in range(CHUNKS):
                pool.wait_ge(s_ln, c + 1)
                pool.tensor_tensor(us3[:, :, 1 + c * CL:1 + (c + 1) * CL],
                                   xp1[:, c * CL:(c + 1) * CL, 0:C].rearrange("p l d -> p d l"),
                                   scale_b, ALU.mult).then_inc(s_us, 1)

            up3 = up.rearrange("p (d s) -> p d s", s=S)

            def make_w(c, k):
                pool.wait_ge(s_h, c * N + k + 1)
                settle(pool)
                pool.tensor_tensor(w_ring[:, k % 4, :].rearrange("p (d s) -> p d s", s=S),
                                   up3[:, bass.ds(c * DC, DC), :],
                                   bc[:, k:k + 1, :].broadcast_to([P, DC, S]), ALU.mult).then_inc(s_w, 1)

            def chunk(c, last):
                for k in range(N):
                    if k + 2 < N:
                        make_w(c, k + 2)
                    elif not last:
                        make_w(c + 1, k + 2 - N)
                    if k not in DVE_HC:
                        pool.wait_ge(s_h, c * N + k + 1 + H_CR)
                        pool.wait_ge(s_add, c * (N + 1) + k - 1 + ADD_CR)
                        pool.tensor_tensor(hc_buf(k), h_buf(k),
                                           bc[:, N + k:N + k + 1, :].broadcast_to([P, DC, S]),
                                           ALU.mult).then_inc(s_hcp, 1)
                pool.wait_ge(s_add, c * (N + 1) + ADD_CR)
                settle(pool)
                pool.tensor_tensor(hh_ring[:, 4, :].rearrange("p (d s) -> p d s", s=S),
                                   us3[:, bass.ds(c * DC, DC), :],
                                   vecs[:, 4, bass.ds(c * DC, DC)].unsqueeze(2).broadcast_to([P, DC, S]),
                                   ALU.mult).then_inc(s_skip, 1)

            pool.wait_ge(s_up, NDC)
            pool.wait_ge(s_bdiv, 1)
            pool.wait_ge(s_us, CHUNKS)
            make_w(0, 0)
            make_w(0, 1)
            with pool.Fori(0, NDC - 1) as c:
                chunk(c, False)
            chunk(NDC - 1, True)

            pool.wait_ge(s_padw, 16)
            pool.wait_ge(s_gate, 2)
            pool.wait_ge(s_xp2, 1)
            for k, rows in enumerate((xp1, xp2)):
                pool.wait_ge(s_slot, k + 1)
                for l in range(L):
                    pool.indirect_dma_start(
                        out=sorted_rows, out_offset=bass.IndirectOffsetOnAxis(ap=slot_i[:, k, l:l + 1], axis=0),
                        in_=rows[:, l, :], in_offset=None).then_inc(s_disp, 16)

            def scatter(k):
                settle(pool)
                for t in range(TPG):
                    pool.indirect_dma_start(
                        out=expert_out, out_offset=bass.IndirectOffsetOnAxis(ap=out_idx[:, k, t:t + 1], axis=0),
                        in_=y_e[:, k, t, :], in_offset=None, bounds_check=PAIRS - 1, oob_is_err=False
                    ).then_inc(s_sc[k], 16)

            with pool.Fori(0, GROUPS // 2) as q:
                for k in range(2):
                    pool.wait_ge(s_idx, 2 * q + k + 1 + ROWS_CR)
                    pool.wait_ge(s_ye, 2 * q + k + 1 + ROWS_CR)
                    scatter(k)
            pool.wait_ge(s_idx, GROUPS + ROWS_CR)
            pool.wait_ge(s_ye, GROUPS + ROWS_CR)
            scatter(0)

        @block.tensor
        def _(pe):
            def x_transposes(g, k):
                pe.wait_ge(s_xready, g + 1)
                t = banks(2 * k, 2)
                for j in range(GL):
                    last = pe.transpose(t[:, j * P:(j + 1) * P],
                                        x_w1[:, (GL * g + 1 + j) * P:(GL * g + 2 + j) * P], ident[:, :])
                last.then_inc(s_xT, 1)

            def conv(g, k):
                o = ps[:, 6 + [0, 1, 0][k], :]
                for j in range(GL + 2):
                    lo, hi = max(j - 2, 0), min(j, GL - 1)
                    m = lo - (j - 2)
                    last = pe.matmul(o[:, lo * C:(hi + 1) * C], xt[:, (GL * g + j) * P:(GL * g + j + 1) * P],
                                     wconv[:, m:m + hi - lo + 1, :],
                                     start=(j == 0), stop=(j == GL + 1), skip_group_check=True)
                last.then_inc(s_conv, 1)

            pe.wait_ge(s_ident, 1)
            pe.wait_ge(s_zero, 4)
            x_transposes(0, 0)
            pe.wait_ge(s_wconv, 3)
            for g in range(NG):
                k = g % GPC
                if g < NG - 1:
                    if g > 0:
                        pe.wait_ge(s_xTc, g)
                    x_transposes(g + 1, (k + 1) % 3)
                pe.wait_ge(s_xTc, min(g + 2, NG))
                if g > 0:
                    pe.wait_ge(s_y, g)
                conv(g, k)

            pe.wait_ge(s_wproj, 16 * 6)
            pe.transpose(ps[0:C + 1, 0, 0:NPROJ], wst[:, :], ident[0:NPROJ, 0:NPROJ]).then_inc(s_wT, 1)
            pe.wait_ge(s_wcat, 1)
            pe.wait_ge(s_y, NG)

            def project(first, weights, width, done, copied):
                for c in range(CHUNKS):
                    pe.wait_ge(s_ln, first + c + 1)
                    if first + c > 0:
                        pe.wait_ge(s_uTc, GPC * (first + c))
                    for k in range(GPC):
                        t = banks(2 * k, 2)
                        for j in range(GL):
                            last = pe.transpose(t[0:C + 1, j * P:(j + 1) * P],
                                                xp1[:, (GPC * c + k) * GL + j, 0:C + 1], ident[:, :])
                        last.then_inc(s_uT, 1)
                    for k in range(GPC):
                        pe.wait_ge(s_uTc, GPC * (first + c) + k + 1)
                        if c + k > 0:
                            pe.wait_ge(copied, GPC * c + k)
                        t = banks(6, 2)
                        for j in range(GL):
                            last = pe.matmul(t[:, j * P:j * P + width], uT[:, k, j * P:(j + 1) * P], weights,
                                             start=True, stop=True)
                        last.then_inc(done, 1)

            project(0, wcat[:, :], NPROJ, s_proj, s_projc)

            pe.wait_ge(s_projc, NG)
            with pe.Fori(0, NDC) as c:
                pe.wait_ge(s_h2, c + H2_CR)
                for k in range(N + 1):
                    if k == N:
                        pe.wait_ge(s_skip, c + 1)
                    elif k in DVE_HC:
                        pe.wait_ge(s_hcv, c * NV + dve_upto(k) + HCV_CR)
                    else:
                        pe.wait_ge(s_hcp, c * NPL + pool_upto(k) + HCP_CR)
                    buf = 4 if k == N else 2 + k % 2
                    for i in range(2):
                        last = pe.matmul(ps[:, i, :], ident[:, :], hh_ring[:, buf, i * BANK:(i + 1) * BANK],
                                         start=(k == 0), stop=False, skip_group_check=True)
                    last.then_inc(s_add, 1)
                half = DC // 2
                for i in range(2):
                    last = pe.matmul(ps[:, i, :].rearrange("p (d s) -> p d s", s=S)[:, :, 1:S], ident[:, :],
                                     hg[:, :, bass.ds(c * DC + i * half, half)].rearrange("p l d -> p d l"),
                                     start=False, stop=True, skip_group_check=True)
                last.then_inc(s_acc, 1)

            pe.wait_ge(s_moew, 16 * 5)
            pe.wait_ge(s_h2, NDC + H2_CR)
            project(CHUNKS, wr[:, :], E, s_lg, s_lgc)

            pe.wait_ge(s_cnt, 2)
            pe.matmul(ps[:, 0, 0:E], ones[:, :], small[:, 1, :], start=True, stop=True).then_inc(s_tot, 1)
            pe.matmul(ps[:, 1, 0:E], tri[:, :], small[:, 1, :], start=True, stop=True).then_inc(s_tot, 1)
            pe.wait_ge(s_te, 2)
            for j in range(2):
                last = pe.transpose(ps[0:1, 2, j * P:(j + 1) * P], tile_e[:, j:j + 1], ident[:, :])
            last.then_inc(s_teT, 1)
            pe.wait_ge(s_tei, 1)
            pe.wait_ge(s_b2, 16)

            def rows_T(g, slot, k, landed):
                pe.wait_ge(s_rows[slot], landed)
                pe.wait_ge(s_rTc, g + 1)
                for t in range(TPG):
                    last = pe.transpose(ps[0:C + 1, k, t * P:(t + 1) * P], rows_in[:, slot, t, 0:C + 1],
                                        ident[:, :])
                last.then_inc(s_rT, 1)

            def experts(g, k):
                es = [pe.value_load(te[0:1, bass.ds(TPG * g + t, 1)], min_val=0, max_val=E - 1)
                      for t in range(TPG)]
                pe.wait_ge(s_rTc, g + 1 + RTC_CR)
                for t in range(TPG):
                    last = pe.matmul(ps[:, 2 + k, t * P:(t + 1) * P], w1_e[:, k, t, :],
                                     xT_e[:, k, t * P:(t + 1) * P], start=True, stop=True)
                last.then_inc(s_hid, 1)
                pe.wait_ge(s_relu, g + 1)
                pe.wait_ge(s_ye, g - 1 + ROWS_CR)
                for t in range(TPG):
                    o = ps[:, 4 + k, t * C:(t + 1) * C]
                    pe.matmul(o, hT_e[:, k, t * P:(t + 1) * P], w2s[:, bass.ds(es[t] * C, C)],
                              start=True, stop=False)
                    last = pe.matmul(o, ones[0:1, :], b2s[:, bass.ds(es[t] * C, C)], start=False, stop=True)
                last.then_inc(s_yps, 1)

            rows_T(0, 0, 0, 16)
            with pe.Fori(0, (GROUPS - 3) // 6) as q:
                for k in range(6):
                    g = 6 * q + k
                    rows_T(g + 1, (k + 1) % 3, (k + 1) % 2, 16 * (2 * q + (k + 1) // 3 + 1))
                    experts(g, k % 2)
            q = (GROUPS - 3) // 6
            for k in range(3):
                g = GROUPS - 3 + k
                if k < 2:
                    rows_T(g + 1, (k + 1) % 3, (k + 1) % 2, 16 * (2 * q + 1))
                experts(g, k % 2)

        @block.scalar
        def _(act):
            act.dma_start(wcol[C:P, 1:2], w[3, 0, :].rearrange("(c a) -> c a", a=1)).then_inc(s_wcol, 16)
            act.dma_start(wcol[0:C, 1:2], w[2, 0, :].rearrange("(c a) -> c a", a=1)).then_inc(s_wcol, 16)
            act.dma_start(wcol[C:P, 2:3], w[1, 0, :].rearrange("(c a) -> c a", a=1)).then_inc(s_wcol, 16)
            act.dma_start(wcol[0:C, 2:3], w[0, 0, :].rearrange("(c a) -> c a", a=1)).then_inc(s_wcol, 16)
            for i, v in enumerate((b, gamma, beta, alpha, D_param, scale)):
                act.dma_start(vecs[:, i, :], v.rearrange("(a c) -> a c", a=1).broadcast_to([P, C])
                              ).then_inc(s_vecs, 16)
            act.dma_start(a_log[:, :], A_log.rearrange("(a c) -> a c", a=1).broadcast_to([P, N])
                          ).then_inc(s_aexp, 16)
            with act.Fori(0, CHUNKS) as c:
                for k in range(GPC):
                    g = GPC * c + k
                    act.wait_ge(s_xT, g + 1)
                    settle(act)
                    act.activation(xt[:, bass.ds((GL * g + 1) * P, GL * P)], banks(2 * k, 2)[:, 0:GL * P],
                                   ACT.Copy).then_inc(s_xTc, 1)
            act.wait_ge(s_wT, 1)
            act.activation(wcat[:, :], ps[0:C + 1, 0, 0:NPROJ], ACT.Copy).then_inc(s_wcat, 1)
            act.wait_ge(s_gnvar, 1)
            act.activation(gn[:, 2:3], gn[:, 1:2], ACT.Sqrt, bias=eps[:, 0:1]).then_inc(s_gnsd, 1)

            def norm_chunk(n):
                act.wait_ge(s_cen, n + 1)
                act.activation(sq, cen, ACT.Square).then_inc(s_sq, 1)
                act.wait_ge(s_var, n + 1)
                act.activation(ln_s[:, 2, :], ln_s[:, 1, :], ACT.Sqrt, scale=1.0 / C, bias=eps[:, 1:2]
                               ).then_inc(s_sd, 1)

            def norm_loop(first):
                with act.Fori(0, CHUNKS) as c:
                    norm_chunk(first + c)
                    for k in range(GPC):
                        g = GPC * (first + c) + k
                        act.wait_ge(s_uT, g + 1)
                        act.activation(uT[:, k, :], banks(2 * k, 2)[0:C + 1, 0:GL * P], ACT.Copy
                                       ).then_inc(s_uTc, 1)

            norm_loop(0)
            act.wait_ge(s_aexp, 16)
            act.activation(a_exp[:, 0, :], a_log[:, :], ACT.Exp).then_inc(s_acols, 1)
            act.wait_ge(s_projc, NG)
            with act.Fori(0, NDC) as c:
                ch = Chain(act, s_act, c * 3)
                t = tmp[:, bass.ds(c * U, U)]
                d = dt[:, bass.ds(c * U, U)]
                settle(act)
                ch.link(act.activation(t, d, ACT.Abs))
                settle(act)
                ch.link(act.activation(t, t, ACT.Exp, scale=-1.0))
                settle(act)
                act.activation(t, t, ACT.Ln, bias=eps[:, 2:3]).then_inc(s_lnp, 1)
                act.wait_ge(s_dt, c + 1)
                settle(act)
                ch.link(act.activation(t, d, ACT.Ln))
                settle(act)
                act.activation(up[:, bass.ds(c * U, U)], t, ACT.Exp, scale=-1.0).then_inc(s_r0, 1)
            act.wait_ge(s_acols, 4)
            with act.Fori(0, NDC) as c:
                for k in range(N):
                    d = dt[:, bass.ds(c * U, U)]
                    act.wait_ge(s_g, c * N + k + G_CR)
                    settle(act)
                    act.activation(banks(6, 2), d, ACT.Tanh, scale=a_exp[:, 2, k:k + 1]).then_inc(s_th, 1)
                    act.wait_ge(s_h, c * N + k - 1 + H_CR)
                    settle(act)
                    act.activation(banks(2 + 2 * (k % 2), 2), d, ACT.Exp, scale=a_exp[:, 1, k:k + 1]
                                   ).then_inc(s_dA, 1)
                act.wait_ge(s_acc, c + 1)
                settle(act)
                act.activation(hg[:, :, bass.ds(c * DC, DC)].rearrange("p l d -> p d l"),
                               banks(0, 2).rearrange("p (d s) -> p d s", s=S)[:, :, 1:S], ACT.Copy
                               ).then_inc(s_h2, 1)
            norm_loop(CHUNKS)
            act.wait_ge(s_ediff, 1)
            act.activation(top[:, 1, :], top[:, 0, :], ACT.Exp).then_inc(s_eexp, 1)
            act.activation(xp2[:, :, 0:C + 1], xp1[:, :, 0:C + 1], ACT.Copy).then_inc(s_xp2, 1)

            def rT_copy(g, k):
                act.wait_ge(s_hid, g - 1 + HID_CR)
                settle(act)
                for t in range(TPG):
                    e = act.value_load(te[0:1, bass.ds(TPG * g + t, 1)], min_val=0, max_val=E - 1)
                    act.activation(w1_e[:, k, t, :], w1s[:, bass.ds(e * HID, HID)], ACT.Copy)
                act.wait_ge(s_rT, g + 1)
                act.activation(xT_e[:, k, :], ps[0:C + 1, k, 0:TPG * P], ACT.Copy).then_inc(s_rTc, 1)

            act.wait_ge(s_moew, 16 * 5)
            act.wait_ge(s_tei, 1)
            with act.Fori(0, GROUPS // 2) as q:
                for k in range(2):
                    rT_copy(2 * q + k, k)
            rT_copy(GROUPS - 1, 0)

        @block.vector
        def _(dve):
            ch = Chain(dve, s_dve)
            dve.memset(x_w1[:, 0:P], 0.0).then_inc(s_zero, 1)
            dve.memset(xt[:, 0:P], 0.0).then_inc(s_zero, 1)
            dve.memset(xt[:, (L + 1) * P:(L + 2) * P], 0.0).then_inc(s_zero, 1)
            dve.memset(x_w1[:, P + T_IN * C:(L + 2) * P], 0.0).then_inc(s_zero, 1)
            for s, n in ((s_h, H_CR), (s_hcv, HCV_CR), (s_hcp, HCP_CR), (s_g, G_CR), (s_h2, H2_CR),  (s_add, ADD_CR), (s_idx, ROWS_CR), (s_ye, ROWS_CR),
                         (s_hid, HID_CR), (s_rTc, RTC_CR), (s_yps, YPS_CR)):
                dve.sem_inc(s, n)
            dve.memset(wcol[C:P, 0:1], 0.0).then_inc(s_dve, 1)
            dve.memset(eps[:, 0:1], EPS_GN).then_inc(s_dve, 1)
            dve.memset(eps[:, 1:2], EPS_LN).then_inc(s_dve, 1)
            dve.memset(eps[:, 2:3], 1.0).then_inc(s_dve, 1)
            dve.memset(dt.rearrange("p (d s) -> p d s", s=S)[:, :, 0:1], DT_RESTART).then_inc(s_dve, 1)
            dve.memset(bc[:, :, 0:1], 0.0).then_inc(s_dve, 1)
            ch.at = 6
            ch.link(dve.memset(xp1[:, :, C:C + 4], 1.0))
            dve.wait_ge(s_wcol, 16 * 5)
            dve.wait_ge(s_pool, 4)
            for m in range(3):
                dve.tensor_scalar(wconv[:, m, :], ident2[:, :], wcol[:, m:m + 1], None, ALU.mult
                                  ).then_inc(s_wconv, 1)
            dve.wait_ge(s_vecs, 16 * 6)
            with dve.Fori(0, CHUNKS) as c:
                for k in range(GPC):
                    g = GPC * c + k
                    dve.wait_ge(s_conv, g + 1)
                    y = hg[:, bass.ds(GL * g, GL), :]
                    dve.tensor_tensor(y, ps[:, 6 + [0, 1, 0][k], 0:GL * C].rearrange("p (l d) -> p l d", d=C),
                                      vecs[:, 0:1, :].broadcast_to([P, GL, C]), ALU.add).then_inc(s_y, 1)
                    dve.wait_ge(s_y, g + 1)
                    dve.bn_stats(stats[:, bass.ds(g, 1), :].rearrange("p a s -> p (a s)"),
                                 y.rearrange("p l d -> p (l d)")).then_inc(s_dve, 1)
            ch.at = 7 + NG
            dve.wait_ge(s_dve, ch.at)
            dve.bn_aggr(gn[:, 0:2], stats[:, :, :].rearrange("p g s -> p (g s)")).then_inc(s_gnvar, 1)
            dve.wait_ge(s_gnsd, 1)
            ch.link(dve.reciprocal(gn[:, 3:4], gn[:, 2:3]))
            start = ch.at

            def b_of(i):
                return vecs[:, i:i + 1, :].broadcast_to([P, CL, C])

            def norm_chunk(n, c):
                h = hg[:, bass.ds(CL * c, CL), :]
                settle(dve)
                ch.link(dve.tensor_reduce(ln_s[:, 0, :], h, AX_X, ALU.add))
                ch.link(dve.tensor_scalar(ln_s[:, 3, :], ln_s[:, 0, :], 1.0 / C, None, ALU.mult))
                dve.tensor_tensor(cen, h, ln_s[:, 3, :].unsqueeze(2).broadcast_to([P, CL, C]), ALU.subtract
                                  ).then_inc(s_cen, 1)
                dve.wait_ge(s_sq, n + 1)
                dve.tensor_reduce(ln_s[:, 1, :], sq, AX_X, ALU.add).then_inc(s_var, 1)
                dve.wait_ge(s_sd, n + 1)
                ch.link(dve.reciprocal(ln_s[:, 0, :], ln_s[:, 2, :]))
                dve.wait_ge(s_cen, n + 1)
                dve.tensor_tensor(xp1[:, bass.ds(CL * c, CL), 0:C], cen,
                                  ln_s[:, 0, :].unsqueeze(2).broadcast_to([P, CL, C]), ALU.mult
                                  ).then_inc(s_ln, 1)
                dve.wait_ge(s_ln, n + 1)

            def proj_copy(g, k):
                dve.wait_ge(s_proj, g + 1)
                t = banks(6, 2)[:, 0:GL * P].rearrange("p (l n) -> p l n", n=P)
                dve.tensor_copy(dt.rearrange("p (d s) -> p d s", s=S)[:, :, bass.ds(1 + GL * g, GL)],
                                t[:, :, 0:C].rearrange("p l n -> p n l")).then_inc(s_dve, 1)
                dve.tensor_copy(bc[:, :, bass.ds(1 + GL * g, GL)],
                                t[:, :, C:NPROJ].rearrange("p l n -> p n l")).then_inc(s_projc, 1)
                ch.at = ch.at + 1

            GN_LN = 4 + 3
            with dve.Fori(0, CHUNKS) as c:
                ch.at = start + c * (GN_LN + GPC)
                h = hg[:, bass.ds(CL * c, CL), :]
                ch.link(dve.scalar_tensor_tensor(out=h, in0=h, scalar=gn[:, 0:1], in1=b_of(1),
                                                 op0=ALU.subtract, op1=ALU.mult))
                ch.link(dve.scalar_tensor_tensor(out=h, in0=h, scalar=gn[:, 3:4], in1=b_of(2),
                                                 op0=ALU.mult, op1=ALU.add))
                ch.link(dve.scalar_tensor_tensor(out=cen, in0=h, scalar=0.0, in1=b_of(3),
                                                 op0=ALU.min, op1=ALU.mult))
                ch.link(dve.scalar_tensor_tensor(out=h, in0=h, scalar=0.0, in1=cen,
                                                 op0=ALU.max, op1=ALU.add))
                norm_chunk(c, c)
                for k in range(GPC):
                    proj_copy(GPC * c + k, k)
            ch.at = start + CHUNKS * (GN_LN + GPC)
            dve.wait_ge(s_projc, NG)
            dve.wait_ge(s_acols, 1)
            dve.tensor_scalar(a_exp[:, 1, :], a_exp[:, 0, :], -1.0, None, ALU.mult).then_inc(s_acols, 1)
            dve.tensor_scalar(a_exp[:, 2, :], a_exp[:, 0, :], -0.5, None, ALU.mult).then_inc(s_acols, 1)
            dve.reciprocal(a_exp[:, 3, :], a_exp[:, 0, :]).then_inc(s_acols, 1)
            dve.wait_ge(s_acols, 4)
            dve.tensor_tensor(bc[:, 0:N, :], bc[:, 0:N, :], a_exp[:, 3, :].unsqueeze(2).broadcast_to([P, N, S]),
                              ALU.mult).then_inc(s_bdiv, 1)
            dve.wait_ge(s_us, CHUNKS)
            start = ch.at
            with dve.Fori(0, NDC) as c:
                ch.at = start + c * 3
                t = tmp[:, bass.ds(c * U, U)]
                d = dt[:, bass.ds(c * U, U)]
                r = up[:, bass.ds(c * U, U)]
                dve.wait_ge(s_lnp, c + 1)
                ch.link(dve.scalar_tensor_tensor(out=d, in0=d, scalar=0.0, in1=t, op0=ALU.max, op1=ALU.add))
                dve.tensor_scalar(d, d, DT_MIN, None, ALU.max).then_inc(s_dt, 1)
                dve.wait_ge(s_r0, c + 1)
                dve.wait_ge(s_dt, c + 1)
                ch.link(dve.tensor_tensor(t, d, r, ALU.mult))
                ch.link(dve.scalar_tensor_tensor(out=t, in0=t, scalar=-2.0, in1=r, op0=ALU.add, op1=ALU.mult))
                dve.tensor_tensor(r, t, us_lg[:, bass.ds(c * U, U)], ALU.mult).then_inc(s_up, 1)
            ch.at = start + NDC * 3

            with dve.Fori(0, NDC) as c:
                for k in range(N):
                    i = c * N + k
                    wv = w_ring[:, k % 4, :]
                    dA = banks(2 + 2 * (k % 2), 2)
                    dve.wait_ge(s_w, i + 1)
                    dve.wait_ge(s_th, i + 1)
                    dve.tensor_tensor(wv, banks(6, 2), wv, ALU.mult).then_inc(s_g, 1)
                    dve.wait_ge(s_dA, i + 1)
                    dve.wait_ge(s_g, i + 1 + G_CR)
                    dve.scalar_tensor_tensor(out=wv, in0=dA, scalar=1.0, in1=wv, op0=ALU.add, op1=ALU.mult
                                             ).then_inc(s_b, 1)
                    if (k - 2) % N in DVE_HC:
                        dve.wait_ge(s_hcv, c * NV + dve_upto(k - 2) + HCV_CR)
                    else:
                        dve.wait_ge(s_hcp, c * NPL + pool_upto(k - 2) + HCP_CR)
                    dve.wait_ge(s_b, i + 1)
                    dve.tensor_tensor_scan(hh_ring[:, k % 2, :], dA, wv, 0.0, ALU.mult, ALU.add
                                           ).then_inc(s_h, 1)
                    if k in DVE_HC:
                        dve.wait_ge(s_h, i + 1 + H_CR)
                        dve.wait_ge(s_add, c * (N + 1) + k - 1 + ADD_CR)
                        dve.tensor_tensor(hc_buf(k), h_buf(k),
                                          bc[:, N + k:N + k + 1, :].broadcast_to([P, DC, S]), ALU.mult
                                          ).then_inc(s_hcv, 1)

            dve.wait_ge(s_h2, NDC + H2_CR)
            start = ch.at
            with dve.Fori(0, CHUNKS) as c:
                ch.at = start + c * 3
                norm_chunk(c + CHUNKS, c)
                for k in range(GPC):
                    g = GPC * c + k
                    dve.wait_ge(s_lg, g + 1)
                    t = banks(6, 2)[:, 0:GL * P].rearrange("p (l n) -> p l n", n=P)
                    dve.tensor_copy(logits[:, bass.ds(GL * g, GL), :], t[:, :, 0:E]).then_inc(s_lgc, 1)
            ch.at = start + CHUNKS * 3
            dve.wait_ge(s_lgc, NG)
            for l in range(L):
                dve.max(mx[:, l, :], logits[:, l, :]).then_inc(s_dve, 1)
            ch.at = ch.at + L
            dve.wait_ge(s_dve, ch.at)
            for l in range(L):
                dve.max_index(mi[:, l, :], mx[:, l, :], logits[:, l, :]).then_inc(s_dve, 1)
            ch.at = ch.at + L
            dve.tensor_tensor(top[:, 0, :], mx[:, :, 1], mx[:, :, 0], ALU.subtract).then_inc(s_ediff, 1)
            dve.wait_ge(s_consts, 5)
            dve.wait_ge(s_dve, ch.at)
            dve.tensor_copy(iota_e[:, :], iota_e_i[:, :]).then_inc(s_dve, 1)
            dve.tensor_copy(tile_no[:, :], tile_no_i[:, :]).then_inc(s_dve, 1)
            dve.tensor_copy(top[:, 2, :], mi[:, :, 0]).then_inc(s_dve, 1)
            ch.at = ch.at + 3
            ch.link(dve.tensor_copy(top[:, 3, :], mi[:, :, 1]))
            ie = iota_e[:, :].unsqueeze(2).broadcast_to([P, E, L])
            for j, m in ((2, mask1), (3, mask2)):
                dve.tensor_tensor(m, ie, top[:, j:j + 1, :].broadcast_to([P, E, L]), ALU.is_equal
                                  ).then_inc(s_dve, 1)
            ch.at = ch.at + 2
            dve.wait_ge(s_dve, ch.at)
            ch.link(dve.tensor_tensor_scan(rank, xt[:, 0:E * L], xt[:, C * S:C * S + E * L], 0.0,
                                           ALU.add, ALU.add))
            upto, cnt = small[:, 0, :], small[:, 1, :]
            ch.link(dve.tensor_copy(upto, rank3[:, :, L - 1]))
            dve.tensor_copy(cnt[:, 0:1], upto[:, 0:1]).then_inc(s_cnt, 1)
            dve.tensor_tensor(cnt[:, 1:E], upto[:, 1:E], upto[:, 0:E - 1], ALU.subtract).then_inc(s_cnt, 1)
            dve.wait_ge(s_tot, 2)
            tiles, ends, before, base, zero = (small[:, i, :] for i in (3, 4, 5, 6, 9))
            dve.memset(zero, 0.0).then_inc(s_dve, 1)
            ch.at = ch.at + 1
            ch.link(dve.tensor_scalar(small_i[:, :], ps[:, 0, 0:E], float(P - 1), None, ALU.add))
            ch.link(dve.tensor_scalar(small_i[:, :], small_i[:, :], P.bit_length() - 1, None,
                                      ALU.logical_shift_right))
            ch.link(dve.tensor_copy(tiles, small_i[:, :]))
            ch.link(dve.tensor_tensor_scan(ends, tiles, zero, 0.0, ALU.add, ALU.add))
            for j in range(2):
                ch.link(dve.tensor_scalar(small[:, 7 + j, :], ends, tile_no[:, j:j + 1], None, ALU.is_le))
                dve.tensor_reduce(tile_e[:, j:j + 1], small[:, 7 + j, :], AX_X, ALU.add).then_inc(s_te, 1)
            ch.link(dve.tensor_tensor(before, ends, tiles, ALU.subtract))
            ch.link(dve.scalar_tensor_tensor(out=before, in0=before, scalar=float(P), in1=ps[:, 1, 0:E],
                                             op0=ALU.mult, op1=ALU.add))
            dve.tensor_scalar(base[:, 0:1], before[:, 0:1], -1.0, None, ALU.add).then_inc(s_dve, 1)
            ch.at = ch.at + 1
            ch.link(dve.scalar_tensor_tensor(out=base[:, 1:E], in0=before[:, 1:E], scalar=-1.0,
                                             in1=upto[:, 0:E - 1], op0=ALU.add, op1=ALU.subtract))
            ch.link(dve.tensor_tensor(rank3, rank3, base.unsqueeze(2).broadcast_to([P, E, L]), ALU.add))
            dve.tensor_copy(xp1[:, :, C + 1:C + 2], slot_i[:, 0, :].unsqueeze(2)).then_inc(s_dve, 1)
            dve.tensor_copy(xp2[:, :, C + 1:C + 2], slot_i[:, 1, :].unsqueeze(2)).then_inc(s_dve, 1)
            dve.memset(xp2[:, :, C + 3:C + 4], 0.0).then_inc(s_dve, 1)
            ch.at = ch.at + 3
            dve.wait_ge(s_eexp, 1)
            ch.link(dve.tensor_scalar(top[:, 4, :], top[:, 1, :], 1.0, None, ALU.add))
            ch.link(dve.reciprocal(top[:, 5, :], top[:, 4, :]))
            dve.tensor_copy(xp1[:, :, C + 2:C + 3], top[:, 5, :].unsqueeze(2)).then_inc(s_gate, 1)
            dve.tensor_tensor(xp2[:, :, C + 2:C + 3], top[:, 1, :].unsqueeze(2), top[:, 5, :].unsqueeze(2),
                              ALU.mult).then_inc(s_gate, 1)
            for k, m in enumerate((mask1, mask2)):
                ch.link(dve.tensor_tensor(m, m, rank3, ALU.mult))
                ch.link(dve.tensor_reduce(top[:, 6, :], m.rearrange("p e l -> p l e"), AX_X, ALU.add))
                dve.tensor_copy(slot_i[:, k, :], top[:, 6, :]).then_inc(s_slot, 1)
                if k == 0:
                    dve.wait_ge(s_slot, 1)
                    dve.wait_ge(s_teT, 1)
                    dve.tensor_scalar(te[:, :], ps[0:1, 2, 0:2 * P], float(E - 1), None, ALU.min
                                      ).then_inc(s_tei, 1)

            def group(g, k, slot, landed, q2):
                dve.wait_ge(s_hid, g + 1 + HID_CR)
                dve.wait_ge(s_yps, g - 1 + YPS_CR)
                dve.tensor_scalar(hT_e[:, k, :], ps[:, 2 + k, 0:TPG * P], 0.0, None, ALU.max
                                  ).then_inc(s_relu, 1)
                dve.wait_ge(s_rows[slot], landed)
                if q2 is not None:
                    dve.wait_ge(s_sc[k], 16 * TPG * q2)
                dve.tensor_copy(out_idx[:, k, :], rows_in[:, slot, :, C + 1]).then_inc(s_idx, 1)
                dve.wait_ge(s_yps, g + 1 + YPS_CR)
                dve.tensor_tensor(y_e[:, k], ps[:, 4 + k, 0:TPG * C].rearrange("p (t d) -> p t d", d=C),
                                  rows_in[:, slot, :, C + 2:C + 3].broadcast_to([P, TPG, C]), ALU.mult
                                  ).then_inc(s_ye, 1)

            for g in range(6):
                group(g, g % 2, g % 3, 16 * (g // 3 + 1), g // 2 or None)
            with dve.Fori(1, (GROUPS - 3) // 6) as q:
                for k in range(6):
                    group(6 * q + k, k % 2, k % 3, 16 * (2 * q + k // 3 + 1), 3 * q + k // 2)
            for k in range(3):
                g = GROUPS - 3 + k
                group(g, k % 2, k, 16 * (g // 3 + 1), g // 2)

            for c in range(CHUNKS):
                h = hg[:, c * CL:(c + 1) * CL, :]
                dve.wait_ge(s_yl[c], 32)
                ch.link(dve.tensor_tensor(h, h, y1[:, c * CL:(c + 1) * CL, :], ALU.add))
                dve.tensor_tensor(h, h, y2[:, c * CL:(c + 1) * CL, :], ALU.add).then_inc(s_fin, 1)


_INS = ["x", "L0_tok_w", "L0_tok_b", "L0_tok_gamma", "L0_tok_beta", "L0_tok_alpha", "L0_attn_A_log",
        "L0_attn_D_param", "L0_attn_scale", "L0_attn_W_dt", "L0_attn_b_dt", "L0_attn_W_B", "L0_attn_b_B",
        "L0_attn_W_C", "L0_attn_b_C", "L0_ffn_Wr", "L0_ffn_br", "L0_ffn_W1", "L0_ffn_b1", "L0_ffn_W2",
        "L0_ffn_b2"]


def kernel(**inputs):
    import numpy as _np
    import concourse.bacc as _bacc
    from concourse import mybir as _mybir
    from concourse.bass_utils import run_bass_kernel_spmd as _run

    nc = _bacc.Bacc("TRN2", target_bir_lowering=False, num_devices=1)
    arrays, args = {}, []
    for name in _INS:
        a = _np.ascontiguousarray(inputs[name])
        arrays[f"in_{name}"] = a
        args.append(nc.dram_tensor(f"in_{name}", a.shape, _mybir.dt.from_np(a.dtype), kind="ExternalInput").ap())
    args.append(nc.dram_tensor("out_dram", (P, L, C), F32, kind="ExternalOutput").ap())
    build(nc, *args)
    r = _run(nc, [arrays], core_ids=[0])
    return r.results[0]["out_dram"]
```

```python
from contextlib import ExitStack

import concourse.bass as bass
from concourse import mybir

F32 = mybir.dt.float32
I32 = mybir.dt.int32
U32 = mybir.dt.uint32
ALU = mybir.AluOpType
ACT = mybir.ActivationFunctionType
ET = mybir.EngineType
AX_X = mybir.AxisListType.X

P = 128
T_IN = 125
C = 64
TAPS = 5
L = 63
GL = 7
NG = L // GL
CHUNKS = 3
GPC = NG // CHUNKS
CL = GL * GPC
N = 16
S = L + 1
DC = 16
NDC = C // DC
U = DC * S
BANK = 512
E = 64
HID = 128
TOK = P * L
PAIRS = 2 * TOK
ROW = 68
TILES = PAIRS // P + E - 1
TPG = 3
GROUPS = TILES // TPG
NOWHERE = 99999.0
EPS_GN = 0.001
EPS_LN = 1e-05
DT_MIN = 1e-19
DT_RESTART = 1e18

NPROJ = C + 2 * N
DVE_HC = (1, 4, 6, 9, 12, 15)
NV = len(DVE_HC)
NPL = N - NV
H_CR, HCV_CR, HCP_CR, ADD_CR, G_CR, H2_CR = 4, 1, 1, 2, 1, 1
RING = 6
ROWS_CR, HID_CR, RTC_CR, YPS_CR = RING, 2, 2, 2


def dve_upto(k):
    return sum(j in DVE_HC for j in range(k + 1)) - sum(j + N in DVE_HC for j in range(k + 1, 0))


def pool_upto(k):
    return k + 1 - dve_upto(k)


class Chain:

    def __init__(self, eng, sem, at=0):
        self.eng, self.sem, self.at = eng, sem, at

    def link(self, ins):
        ins.then_inc(self.sem, 1)
        self.at = self.at + 1
        self.eng.wait_ge(self.sem, self.at)


def build(nc, x, w, b, gamma, beta, alpha, A_log, D_param, scale, W_dt, b_dt, W_B, b_B, W_C, b_C,
          Wr, br, W1, b1, W2, b2, out):
    sorted_rows = nc.dram_tensor("sorted_rows", (TILES * P, ROW), F32, kind="Internal").ap()
    expert_out = nc.dram_tensor("expert_out", (PAIRS, C), F32, kind="Internal").ap()

    with ExitStack() as ctx:
        def sb(name, shape, dt=F32):
            return ctx.enter_context(nc.sbuf_tensor(name, shape, dt))

        def sem(name):
            return ctx.enter_context(nc.semaphore(name))

        XPAIRS = L + 2
        x_w1 = sb("x_w1", [P, XPAIRS * P])
        hg = sb("hg", [P, L, C])
        xp1 = sb("xp1", [P, L, ROW])
        dt_xp2 = sb("dt_xp2", [P, L * ROW])
        xt = sb("xt", [P, XPAIRS * P])
        us_lg = sb("us_lg", [P, C * S])
        bc = sb("bc", [P, 2 * N, S])
        w2s = sb("w2s", [P, E * C])
        w_ring = sb("w_ring", [P, 4, U])
        hh_ring = sb("hh_ring", [P, 5, U])
        ident = sb("ident", [P, P])
        ident2 = sb("ident2", [P, C])
        ones = sb("ones", [P, P])
        tri = sb("tri", [P, P])
        wconv = sb("wconv", [P, 3, C])
        wcol = sb("wcol", [P, 3])
        wst = sb("wst", [NPROJ, C + 1])
        wcat = sb("wcat", [C + 1, NPROJ])
        wr = sb("wr", [C + 1, E])
        vecs = sb("vecs", [P, 6, C])
        a_log = sb("a_log", [P, N])
        a_exp = sb("a_exp", [P, 4, N])
        eps = sb("eps", [P, 3])
        stats = sb("stats", [P, NG, 6])
        gn = sb("gn", [P, 4])
        ln_s = sb("ln_s", [P, 4, CL])
        pad_rows = sb("pad_rows", [P, TPG, ROW])
        mx = sb("mx", [P, L, 8])
        mi = sb("mi", [P, L, 8], U32)
        top = sb("top", [P, 7, L])
        iota_e = sb("iota_e", [P, E])
        iota_e_i = sb("iota_e_i", [P, E], I32)
        small = sb("small", [P, 10, E])
        small_i = sb("small_i", [P, E], I32)
        slot_i = sb("slot_i", [P, 2, L], I32)
        tile_no_i = sb("tile_no_i", [P, 2], I32)
        tile_no = sb("tile_no", [P, 2])
        tile_e = sb("tile_e", [P, 2])
        te = sb("te", [1, 2 * P], I32)
        out_idx = sb("out_idx", [P, 2, TPG], I32)

        uT = xt[0:C + 1, 0:3 * GL * P].rearrange("p (k n) -> p k n", k=3)
        dt = dt_xp2[:, 0:C * S]
        xp2 = dt_xp2[:, :].rearrange("p (l r) -> p l r", r=ROW)
        tmp = xt[:, 0:C * S]
        up = xt[:, C * S:2 * C * S]
        us3 = us_lg[:, :].rearrange("p (d s) -> p d s", s=S)
        logits = us_lg[:, 0:L * E].rearrange("p (l e) -> p l e", e=E)
        hh_flat = hh_ring[:, :, :].rearrange("p k n -> p (k n)")
        gtmp = hh_flat[:, 0:CL * C].rearrange("p (l d) -> p l d", d=C)
        mask1 = hh_flat[:, 0:E * L].rearrange("p (e l) -> p e l", l=L)
        mask2 = xt[:, C * S:C * S + E * L].rearrange("p (e l) -> p e l", l=L)
        w_flat = w_ring[:, :, :].rearrange("p k n -> p (k n)")
        b2s = w_flat[:, 0:E * C]
        cen = w_flat[:, 0:2 * CL * C].rearrange("p (k l d) -> p k l d", k=2, d=C)
        sq = w_flat[:, 2 * CL * C:3 * CL * C].rearrange("p (l d) -> p l d", d=C)
        rank = xt[:, 0:E * L]
        rank3 = rank.rearrange("p (e l) -> p e l", l=L)
        w1s = x_w1[0:C + 1, 0:E * HID]
        o = 0
        rows_in = us_lg[:, 0:RING * TPG * ROW].rearrange("p (k t r) -> p k t r", k=RING, r=ROW)
        o += RING * TPG * ROW
        xT_e = us_lg[0:C + 1, o:o + 2 * TPG * P].rearrange("p (k n) -> p k n", k=2)
        o += 2 * TPG * P
        hT_e = us_lg[:, o:o + 2 * TPG * P].rearrange("p (k n) -> p k n", k=2)
        o += 2 * TPG * P
        y_e = us_lg[:, o:o + 2 * TPG * C].rearrange("p (k t d) -> p k t d", k=2, d=C)
        o += 2 * TPG * C
        w1_e = us_lg[0:C + 1, o:o + 2 * TPG * HID].rearrange("p (k t n) -> p k t n", k=2, n=HID)
        y1 = xt[:, 0:L * C].rearrange("p (l d) -> p l d", d=C)
        y2 = xt[:, L * C:2 * L * C].rearrange("p (l d) -> p l d", d=C)

        ps = ctx.enter_context(nc.psum_tensor("ps", [P, 8, BANK], F32))

        def banks(a, n):
            return ps[:, a:a + n, :].rearrange("p k n -> p (k n)")

        s_x = [sem(f"s_x{g}") for g in range(NG)]
        s_settled = sem("s_settled")
        s_xready = sem("s_xready")
        s_vecs = sem("s_vecs")
        s_wcol = sem("s_wcol")
        s_wproj = sem("s_wproj")
        s_moew = sem("s_moew")
        s_b2 = sem("s_b2")
        s_padw = sem("s_padw")
        s_zero = sem("s_zero")
        s_pool = sem("s_pool")
        s_ident = sem("s_ident")
        s_consts = sem("s_consts")
        s_wconv = sem("s_wconv")
        s_xT = sem("s_xT")
        s_xTc = sem("s_xTc")
        s_conv = sem("s_conv")
        s_y = sem("s_y")
        s_wT = sem("s_wT")
        s_wcat = sem("s_wcat")
        s_dve = sem("s_dve")
        s_act = sem("s_act")
        s_gnvar = sem("s_gnvar")
        s_gnsd = sem("s_gnsd")
        s_cen = sem("s_cen")
        s_sq = sem("s_sq")
        s_var = sem("s_var")
        s_sd = sem("s_sd")
        s_ln = sem("s_ln")
        s_uT = sem("s_uT")
        s_uTc = sem("s_uTc")
        s_proj = sem("s_proj")
        s_projc = sem("s_projc")
        s_us = sem("s_us")
        s_aexp = sem("s_aexp")
        s_acols = sem("s_acols")
        s_bdiv = sem("s_bdiv")
        s_lnp = sem("s_lnp")
        s_dt = sem("s_dt")
        s_r0 = sem("s_r0")
        s_up = sem("s_up")
        s_w = sem("s_w")
        s_th = sem("s_th")
        s_dA = sem("s_dA")
        s_g = sem("s_g")
        s_b = sem("s_b")
        s_h = sem("s_h")
        s_hcv = sem("s_hcv")
        s_hcp = sem("s_hcp")
        s_skip = sem("s_skip")
        s_add = sem("s_add")
        s_h2 = sem("s_h2")
        s_lg = sem("s_lg")
        s_lgc = sem("s_lgc")
        s_ediff = sem("s_ediff")
        s_eexp = sem("s_eexp")
        s_gate = sem("s_gate")
        s_xp2 = sem("s_xp2")
        s_cnt = sem("s_cnt")
        s_tot = sem("s_tot")
        s_te = sem("s_te")
        s_teT = sem("s_teT")
        s_tei = sem("s_tei")
        s_slot = sem("s_slot")
        s_disp = sem("s_disp")
        s_rows = [sem(f"s_rows{k}") for k in range(RING)]
        s_rT = sem("s_rT")
        s_rTc = sem("s_rTc")
        s_hid = sem("s_hid")
        s_relu = sem("s_relu")
        s_yps = sem("s_yps")
        s_yb = sem("s_yb")
        s_ye = sem("s_ye")
        s_idx = sem("s_idx")
        s_sc = [sem(f"s_sc{k}") for k in range(2)]
        s_yl = [sem(f"s_yl{k}") for k in range(CHUNKS)]
        s_fin = sem("s_fin")
        s_out = sem("s_out")

        def h_buf(k):
            return hh_ring[:, k % 2, :].rearrange("p (d s) -> p d s", s=S)

        def hc_buf(k):
            return hh_ring[:, 2 + k % 2, :].rearrange("p (d s) -> p d s", s=S)

        def settle(eng):
            eng.sem_inc(s_settled, 1)

        def experts(engine, g):
            return nc.values_load_multi_w_load_instructions(te[0:1, bass.ds(4 * g, 4)], engines=[engine],
                                                            min_val=0, max_val=E - 1, skip_runtime_bounds_check_because=
                                                            "te is a count of experts, clamped to E - 1")[1]

        block = ctx.enter_context(nc.Block())

        @block.sync
        def _(sp):
            flat = x.rearrange("b t c -> b (t c)")
            cut = [0] + [min((2 * GL * (g + 1) + 2), T_IN) for g in range(NG - 1)] + [T_IN]
            sp.dma_start(wcol[0:C, 0:1], w[4, 0, :].rearrange("(c a) -> c a", a=1)).then_inc(s_wcol, 16)
            for g in range(NG):
                a, z = cut[g] * C, cut[g + 1] * C
                sp.dma_start(x_w1[:, P + a:P + z], flat[:, a:z]).then_inc(s_x[g], 16)
            sp.dma_start(wst[0:C, 0:C], W_dt).then_inc(s_wproj, 16)
            sp.dma_start(wst[C:C + N, 0:C], W_B).then_inc(s_wproj, 16)
            sp.dma_start(wst[C + N:NPROJ, 0:C], W_C).then_inc(s_wproj, 16)
            sp.dma_start(wst[0:C, C:C + 1], b_dt.rearrange("(c a) -> c a", a=1)).then_inc(s_wproj, 16)
            sp.dma_start(wst[C:C + N, C:C + 1], b_B.rearrange("(c a) -> c a", a=1)).then_inc(s_wproj, 16)
            sp.dma_start(wst[C + N:NPROJ, C:C + 1], b_C.rearrange("(c a) -> c a", a=1)).then_inc(s_wproj, 16)
            for g in range(NG):
                sp.wait_ge(s_x[g], 16)
                sp.sem_inc(s_xready, 1)
            sp.wait_ge(s_pool, 7)
            sp.dma_start(sorted_rows.rearrange("(p k t) r -> p k (t r)", p=P, t=TPG),
                         pad_rows[:, :, :].rearrange("p t r -> p (t r)").unsqueeze(1).broadcast_to(
                             [P, GROUPS, TPG * ROW])).then_inc(s_padw, 16)
            sp.dma_start(w2s[:, :].rearrange("k (e d) -> k e d", e=E), W2.rearrange("e k d -> k e d")
                         ).then_inc(s_moew, 16)
            sp.dma_start(wr[0:C, :], Wr).then_inc(s_moew, 16)
            sp.dma_start(wr[C:C + 1, :], br.rearrange("(a e) -> a e", a=1)).then_inc(s_moew, 16)
            sp.wait_ge(s_xT, NG)
            sp.dma_start(w1s[0:C, :].rearrange("k (e h) -> k e h", e=E), W1.rearrange("e k h -> k e h")
                         ).then_inc(s_moew, 16)
            sp.dma_start(w1s[C:C + 1, :], b1.rearrange("(a e) h -> a (e h)", a=1)).then_inc(s_moew, 16)
            sp.wait_ge(s_ln, 2 * CHUNKS)
            sp.dma_start(b2s, b2.rearrange("(a e) d -> a (e d)", a=1).broadcast_to([P, E * C])).then_inc(s_b2, 16)
            sp.wait_ge(s_disp, 16 * 2 * L)

            def load_rows(g, k):
                sp.wait_ge(s_idx, g + 1)
                sp.wait_ge(s_ye, g + 1)
                sp.dma_start(rows_in[:, k], sorted_rows[bass.ds(g * (TPG * P), TPG * P), :].rearrange(
                    "(t p) r -> p t r", t=TPG)).then_inc(s_rows[k], 16)

            with sp.Fori(0, GROUPS // RING) as q:
                for k in range(RING):
                    load_rows(RING * q + k, k)
            for k in range(GROUPS % RING):
                load_rows(GROUPS - GROUPS % RING + k, k)
            for k in range(2):
                sp.wait_ge(s_sc[k], 16 * TPG * ((GROUPS + 1 - k) // 2))
            eo = expert_out.rearrange("(k b l) d -> k b l d", k=2, l=L)
            for c in range(CHUNKS):
                for k, y in enumerate((y1, y2)):
                    sp.dma_start(y[:, c * CL:(c + 1) * CL, :], eo[k, :, c * CL:(c + 1) * CL, :]
                                 ).then_inc(s_yl[c], 16)
            for c in range(CHUNKS):
                sp.wait_ge(s_fin, c + 1)
                sp.dma_start(out[:, c * CL:(c + 1) * CL, :], hg[:, c * CL:(c + 1) * CL, :]
                             ).then_inc(s_out, 16)
            sp.wait_ge(s_out, 16 * CHUNKS)

        @block.gpsimd
        def _(pool):
            ch = Chain(pool, s_pool)
            ch.link(pool.memset(ident[:, :], 0.0))
            ch.link(pool.memset(ident2[:, :], 0.0))
            pool.affine_select(out=ident[:, :], in_=ident[:, :], compare_op=ALU.not_equal, fill=1.0, base=0,
                               pattern=[[-1, P]], channel_multiplier=1).then_inc(s_ident, 1)
            for s in range(2):
                ch.link(pool.affine_select(out=ident2[:, :], in_=ident2[:, :], compare_op=ALU.not_equal,
                                           fill=1.0, base=-C * s, pattern=[[-1, C]], channel_multiplier=1))
            ch.link(pool.memset(pad_rows[:, :, :], 0.0))
            ch.link(pool.memset(pad_rows[:, :, C:C + 1], 1.0))
            ch.link(pool.memset(pad_rows[:, :, C + 1:C + 2], NOWHERE))
            ch.link(pool.memset(ones[:, :], 1.0))
            ch.link(pool.memset(tri[:, :], 1.0))
            ch.link(pool.affine_select(out=tri[:, :], in_=tri[:, :], compare_op=ALU.is_gt, fill=0.0, base=0,
                                       pattern=[[1, P]], channel_multiplier=-1))
            pool.iota(iota_e_i[:, :], [[1, E]], base=0, channel_multiplier=0).then_inc(s_consts, 1)
            pool.iota(tile_no_i[:, :], [[P, 2]], base=0, channel_multiplier=1).then_inc(s_consts, 1)
            pool.iota(slot_i[:, 0, :], [[1, L]], base=0, channel_multiplier=L).then_inc(s_consts, 1)
            pool.iota(slot_i[:, 1, :], [[1, L]], base=TOK, channel_multiplier=L).then_inc(s_consts, 1)
            pool.memset(us3[:, :, 0:1], 0.0).then_inc(s_consts, 1)
            scale_b = vecs[:, 5, :].unsqueeze(2).broadcast_to([P, C, CL])
            pool.wait_ge(s_vecs, 16 * 6)
            for c in range(CHUNKS):
                pool.wait_ge(s_ln, c + 1)
                pool.tensor_tensor(us3[:, :, 1 + c * CL:1 + (c + 1) * CL],
                                   xp1[:, c * CL:(c + 1) * CL, 0:C].rearrange("p l d -> p d l"),
                                   scale_b, ALU.mult).then_inc(s_us, 1)

            up3 = up.rearrange("p (d s) -> p d s", s=S)

            def make_w(c, k):
                if k == 0:
                    pool.wait_ge(s_up, c + 1)
                pool.wait_ge(s_h, c * N + k + 1)
                settle(pool)
                pool.tensor_tensor(w_ring[:, k % 4, :].rearrange("p (d s) -> p d s", s=S),
                                   up3[:, bass.ds(c * DC, DC), :],
                                   bc[:, k:k + 1, :].broadcast_to([P, DC, S]), ALU.mult).then_inc(s_w, 1)

            def chunk(c, last):
                pool.wait_ge(s_add, c * (N + 1) + ADD_CR)
                settle(pool)
                pool.tensor_tensor(hh_ring[:, 4, :].rearrange("p (d s) -> p d s", s=S),
                                   us3[:, bass.ds(c * DC, DC), :],
                                   vecs[:, 4, bass.ds(c * DC, DC)].unsqueeze(2).broadcast_to([P, DC, S]),
                                   ALU.mult).then_inc(s_skip, 1)
                for k in range(N):
                    if k + 2 < N:
                        make_w(c, k + 2)
                    elif not last:
                        make_w(c + 1, k + 2 - N)
                    if k not in DVE_HC:
                        pool.wait_ge(s_h, c * N + k + 1 + H_CR)
                        pool.wait_ge(s_add, c * (N + 1) + k + ADD_CR)
                        pool.tensor_tensor(hc_buf(k), h_buf(k),
                                           bc[:, N + k:N + k + 1, :].broadcast_to([P, DC, S]),
                                           ALU.mult).then_inc(s_hcp, 1)

            pool.wait_ge(s_bdiv, 1)
            pool.wait_ge(s_us, CHUNKS)
            make_w(0, 0)
            make_w(0, 1)
            with pool.Fori(0, NDC - 1) as c:
                chunk(c, False)
            chunk(NDC - 1, True)

            pool.wait_ge(s_padw, 16)
            pool.wait_ge(s_gate, 2)
            pool.wait_ge(s_xp2, 1)
            for k, rows in enumerate((xp1, xp2)):
                for l in range(L):
                    if l % CL == 0:
                        pool.wait_ge(s_slot, CHUNKS * k + l // CL + 1)
                    pool.indirect_dma_start(
                        out=sorted_rows, out_offset=bass.IndirectOffsetOnAxis(ap=slot_i[:, k, l:l + 1], axis=0),
                        in_=rows[:, l, :], in_offset=None).then_inc(s_disp, 16)

            def scatter(k):
                settle(pool)
                for t in range(TPG):
                    pool.indirect_dma_start(
                        out=expert_out, out_offset=bass.IndirectOffsetOnAxis(ap=out_idx[:, k, t:t + 1], axis=0),
                        in_=y_e[:, k, t, :], in_offset=None, bounds_check=PAIRS - 1, oob_is_err=False
                    ).then_inc(s_sc[k], 16)

            with pool.Fori(0, GROUPS // 2) as q:
                for k in range(2):
                    pool.wait_ge(s_idx, 2 * q + k + 1 + ROWS_CR)
                    pool.wait_ge(s_ye, 2 * q + k + 1 + ROWS_CR)
                    scatter(k)
            pool.wait_ge(s_idx, GROUPS + ROWS_CR)
            pool.wait_ge(s_ye, GROUPS + ROWS_CR)
            scatter(0)

        @block.tensor
        def _(pe):
            def x_transposes(g, k):
                pe.wait_ge(s_xready, g + 1)
                t = banks(2 * k, 2)
                for j in range(GL):
                    last = pe.transpose(t[:, j * P:(j + 1) * P],
                                        x_w1[:, (GL * g + 1 + j) * P:(GL * g + 2 + j) * P], ident[:, :])
                last.then_inc(s_xT, 1)

            def conv(g, k):
                o = ps[:, 6 + [0, 1, 0][k], :]
                for j in range(GL + 2):
                    lo, hi = max(j - 2, 0), min(j, GL - 1)
                    m = lo - (j - 2)
                    last = pe.matmul(o[:, lo * C:(hi + 1) * C], xt[:, (GL * g + j) * P:(GL * g + j + 1) * P],
                                     wconv[:, m:m + hi - lo + 1, :],
                                     start=(j == 0), stop=(j == GL + 1), skip_group_check=True)
                last.then_inc(s_conv, 1)

            pe.wait_ge(s_ident, 1)
            pe.wait_ge(s_zero, 4)
            x_transposes(0, 0)
            x_transposes(1, 1)
            pe.wait_ge(s_wconv, 3)
            for g in range(NG):
                k = g % GPC
                if g < NG - 2:
                    if g > 0:
                        pe.wait_ge(s_xTc, g)
                    x_transposes(g + 2, (k + 2) % 3)
                pe.wait_ge(s_xTc, min(g + 2, NG))
                if g > 0:
                    pe.wait_ge(s_y, g)
                conv(g, k)

            pe.wait_ge(s_wproj, 16 * 6)
            pe.transpose(ps[0:C + 1, 0, 0:NPROJ], wst[:, :], ident[0:NPROJ, 0:NPROJ]).then_inc(s_wT, 1)
            pe.wait_ge(s_wcat, 1)
            pe.wait_ge(s_y, NG)

            def project(first, weights, width, pitch, behind, done, copied):
                for c in range(CHUNKS):
                    pe.wait_ge(s_ln, first + c + 1)
                    if first + c > 0:
                        pe.wait_ge(s_uTc, GPC * (first + c))
                    for k in range(GPC):
                        if behind == GPC and c > 0 and k + 1 < GPC:
                            pe.wait_ge(copied, GPC * (c - 1) + k + 2)
                        t = banks(2 * k, 2)
                        for j in range(GL):
                            last = pe.transpose(t[0:C + 1, j * P:(j + 1) * P],
                                                xp1[:, (GPC * c + k) * GL + j, 0:C + 1], ident[:, :])
                        last.then_inc(s_uT, 1)
                    for k in range(GPC):
                        pe.wait_ge(s_uTc, GPC * (first + c) + k + 1)
                        g = GPC * c + k
                        if g >= behind:
                            pe.wait_ge(copied, g - behind + 1)
                        t = banks((2 * k + 6) % 8, 2) if behind == GPC else ps[:, 6 + g % 2, :]
                        for j in range(GL):
                            last = pe.matmul(t[:, j * pitch:j * pitch + width], uT[:, k, j * P:(j + 1) * P], weights,
                                             start=True, stop=True)
                        last.then_inc(done, 1)

            project(0, wcat[:, :], NPROJ, P, GPC, s_proj, s_projc)

            pe.wait_ge(s_projc, NG)
            with pe.Fori(0, NDC) as c:
                pe.wait_ge(s_h2, c + H2_CR)
                half = DC // 2
                for k in range(-1, N):
                    if k < 0:
                        pe.wait_ge(s_skip, c + 1)
                    elif k in DVE_HC:
                        pe.wait_ge(s_hcv, c * NV + dve_upto(k) + HCV_CR)
                    else:
                        pe.wait_ge(s_hcp, c * NPL + pool_upto(k) + HCP_CR)
                    buf = 4 if k < 0 else 2 + k % 2
                    for i in range(2):
                        last = pe.matmul(ps[:, i, :], ident[:, :], hh_ring[:, buf, i * BANK:(i + 1) * BANK],
                                         start=(k < 0), stop=(k == N - 1), skip_group_check=True)
                    last.then_inc(s_add, 1)
                    if k < 0:
                        for i in range(2):
                            pe.matmul(ps[:, i, :].rearrange("p (d s) -> p d s", s=S)[:, :, 1:S], ident[:, :],
                                      hg[:, :, bass.ds(c * DC + i * half, half)].rearrange("p l d -> p d l"),
                                      start=False, stop=False, skip_group_check=True)

            pe.wait_ge(s_moew, 16 * 5)
            pe.wait_ge(s_h2, NDC + H2_CR)
            project(CHUNKS, wr[:, :], E, E, 2, s_lg, s_lgc)

            pe.wait_ge(s_cnt, 2)
            pe.matmul(ps[:, 0, 0:E], ones[:, :], small[:, 1, :], start=True, stop=True).then_inc(s_tot, 1)
            pe.matmul(ps[:, 1, 0:E], tri[:, :], small[:, 1, :], start=True, stop=True).then_inc(s_tot, 1)
            pe.wait_ge(s_te, 2)
            for j in range(2):
                last = pe.transpose(ps[0:1, 2, j * P:(j + 1) * P], tile_e[:, j:j + 1], ident[:, :])
            last.then_inc(s_teT, 1)
            pe.wait_ge(s_tei, 1)

            def rows_T(g, slot, k, landed):
                pe.wait_ge(s_rows[slot], landed)
                pe.wait_ge(s_rTc, g + 1)
                for t in range(TPG):
                    last = pe.transpose(ps[0:C + 1, k, t * P:(t + 1) * P], rows_in[:, slot, t, 0:C + 1],
                                        ident[:, :])
                last.then_inc(s_rT, 1)

            def hidden(g, k):
                pe.wait_ge(s_rTc, g + 1 + RTC_CR)
                for t in range(TPG):
                    last = pe.matmul(ps[:, 2 + k, t * P:(t + 1) * P], w1_e[:, k, t, :],
                                     xT_e[:, k, t * P:(t + 1) * P], start=True, stop=True)
                last.then_inc(s_hid, 1)

            def outputs(g, k):
                es = experts(ET.PE, g)
                pe.wait_ge(s_relu, g + 1)
                pe.wait_ge(s_ye, g - 1 + ROWS_CR)
                for t in range(TPG):
                    last = pe.matmul(ps[:, 4 + k, t * C:(t + 1) * C], hT_e[:, k, t * P:(t + 1) * P],
                                     w2s[:, bass.ds(es[t] * C, C)], start=True, stop=True)
                last.then_inc(s_yps, 1)

            rows_T(0, 0, 0, 16)
            rows_T(1, 1, 1, 16)
            hidden(0, 0)
            with pe.Fori(0, GROUPS // RING) as q:
                for k in range(RING):
                    g = RING * q + k
                    rows_T(g + 2, (k + 2) % RING, k % 2, 16 * (q + (k + 2) // RING + 1))
                    hidden(g + 1, (k + 1) % 2)
                    outputs(g, k % 2)
            for g in range(GROUPS - GROUPS % RING, GROUPS):
                if g + 2 < GROUPS:
                    rows_T(g + 2, (g + 2) % RING, g % 2, 16 * ((g + 2) // RING + 1))
                if g + 1 < GROUPS:
                    hidden(g + 1, (g + 1) % 2)
                outputs(g, g % 2)

        @block.scalar
        def _(act):
            act.dma_start(wcol[C:P, 1:2], w[3, 0, :].rearrange("(c a) -> c a", a=1)).then_inc(s_wcol, 16)
            act.dma_start(wcol[0:C, 1:2], w[2, 0, :].rearrange("(c a) -> c a", a=1)).then_inc(s_wcol, 16)
            act.dma_start(wcol[C:P, 2:3], w[1, 0, :].rearrange("(c a) -> c a", a=1)).then_inc(s_wcol, 16)
            act.dma_start(wcol[0:C, 2:3], w[0, 0, :].rearrange("(c a) -> c a", a=1)).then_inc(s_wcol, 16)
            for i, v in enumerate((b, gamma, beta, alpha, D_param, scale)):
                act.dma_start(vecs[:, i, :], v.rearrange("(a c) -> a c", a=1).broadcast_to([P, C])
                              ).then_inc(s_vecs, 16)
            act.dma_start(a_log[:, :], A_log.rearrange("(a c) -> a c", a=1).broadcast_to([P, N])
                          ).then_inc(s_aexp, 16)
            with act.Fori(0, CHUNKS) as c:
                for k in range(GPC):
                    g = GPC * c + k
                    act.wait_ge(s_xT, g + 1)
                    settle(act)
                    act.activation(xt[:, bass.ds((GL * g + 1) * P, GL * P)], banks(2 * k, 2)[:, 0:GL * P],
                                   ACT.Copy).then_inc(s_xTc, 1)
            act.wait_ge(s_wT, 1)
            act.activation(wcat[:, :], ps[0:C + 1, 0, 0:NPROJ], ACT.Copy).then_inc(s_wcat, 1)
            act.wait_ge(s_gnvar, 1)
            act.activation(gn[:, 2:3], gn[:, 1:2], ACT.Sqrt, bias=eps[:, 0:1]).then_inc(s_gnsd, 1)

            def square(n):
                act.wait_ge(s_cen, n + 1)
                if n > 0:
                    act.wait_ge(s_var, n)
                act.activation(sq, cen[:, n % 2], ACT.Square).then_inc(s_sq, 1)

            def deviation(n):
                act.wait_ge(s_var, n + 1)
                act.activation(ln_s[:, 2, :], ln_s[:, 1, :], ACT.Sqrt, scale=1.0 / C, bias=eps[:, 1:2]
                               ).then_inc(s_sd, 1)

            def uT_copies(n):
                for k in range(GPC):
                    act.wait_ge(s_uT, GPC * n + k + 1)
                    act.activation(uT[:, k, :], banks(2 * k, 2)[0:C + 1, 0:GL * P], ACT.Copy
                                   ).then_inc(s_uTc, 1)

            for n in range(CHUNKS):
                square(n)
                if n > 0:
                    uT_copies(n - 1)
                deviation(n)
            uT_copies(CHUNKS - 1)
            act.wait_ge(s_aexp, 16)
            act.activation(a_exp[:, 0, :], a_log[:, :], ACT.Exp).then_inc(s_acols, 1)
            act.wait_ge(s_projc, NG)
            ch = Chain(act, s_act)
            parts = [[v[:, c * U:(c + 1) * U] for v in (tmp, dt, up)] for c in range(NDC)]
            for t, d, r in parts:
                ch.link(act.activation(t, d, ACT.Abs))
                ch.link(act.activation(t, t, ACT.Exp, scale=-1.0))
            for t, d, r in parts:
                act.activation(t, t, ACT.Ln, bias=eps[:, 2:3]).then_inc(s_lnp, 1)
            for c, (t, d, r) in enumerate(parts):
                act.wait_ge(s_dt, c + 1)
                ch.link(act.activation(t, d, ACT.Ln))
            for t, d, r in parts:
                act.activation(r, t, ACT.Exp, scale=-1.0).then_inc(s_r0, 1)
            act.wait_ge(s_acols, 4)
            def sum_out(c):
                act.wait_ge(s_add, (c + 1) * (N + 1) + ADD_CR)
                settle(act)
                act.activation(hg[:, :, bass.ds(c * DC, DC)].rearrange("p l d -> p d l"),
                               banks(0, 2).rearrange("p (d s) -> p d s", s=S)[:, :, 1:S], ACT.Copy
                               ).then_inc(s_h2, 1)

            def exps(c, behind):
                for k in range(N):
                    d = dt[:, bass.ds(c * U, U)]
                    act.wait_ge(s_g, c * N + k + G_CR)
                    settle(act)
                    act.activation(banks(6, 2), d, ACT.Tanh, scale=a_exp[:, 2, k:k + 1]).then_inc(s_th, 1)
                    act.wait_ge(s_h, c * N + k - 1 + H_CR)
                    settle(act)
                    act.activation(banks(2 + 2 * (k % 2), 2), d, ACT.Exp, scale=a_exp[:, 1, k:k + 1]
                                   ).then_inc(s_dA, 1)
                    if k == 2 and behind:
                        sum_out(c - 1)

            exps(0, False)
            with act.Fori(1, NDC) as c:
                exps(c, True)
            sum_out(NDC - 1)
            square(CHUNKS)
            deviation(CHUNKS)
            for n in range(CHUNKS + 1, 2 * CHUNKS):
                square(n)
                if n > CHUNKS + 1:
                    uT_copies(n - 2)
                deviation(n)
            uT_copies(2 * CHUNKS - 2)
            uT_copies(2 * CHUNKS - 1)
            act.wait_ge(s_ediff, CHUNKS)
            act.activation(top[:, 1, :], top[:, 0, :], ACT.Exp).then_inc(s_eexp, 1)
            act.activation(xp2[:, :, 0:C + 1], xp1[:, :, 0:C + 1], ACT.Copy).then_inc(s_xp2, 1)

            def rT_copy(g, k):
                es = experts(ET.Activation, g)
                act.wait_ge(s_hid, g - 1 + HID_CR)
                settle(act)
                for t in range(TPG):
                    act.activation(w1_e[:, k, t, :], w1s[:, bass.ds(es[t] * HID, HID)], ACT.Copy)
                act.wait_ge(s_rT, g + 1)
                act.activation(xT_e[:, k, :], ps[0:C + 1, k, 0:TPG * P], ACT.Copy).then_inc(s_rTc, 1)

            act.wait_ge(s_moew, 16 * 5)
            act.wait_ge(s_tei, 1)
            with act.Fori(0, GROUPS // 2) as q:
                for k in range(2):
                    rT_copy(2 * q + k, k)
            rT_copy(GROUPS - 1, 0)

        @block.vector
        def _(dve):
            ch = Chain(dve, s_dve)
            dve.memset(x_w1[:, 0:P], 0.0).then_inc(s_zero, 1)
            dve.memset(xt[:, 0:P], 0.0).then_inc(s_zero, 1)
            dve.memset(xt[:, (L + 1) * P:(L + 2) * P], 0.0).then_inc(s_zero, 1)
            dve.memset(x_w1[:, P + T_IN * C:(L + 2) * P], 0.0).then_inc(s_zero, 1)
            for s, n in ((s_h, H_CR), (s_hcv, HCV_CR), (s_hcp, HCP_CR), (s_g, G_CR), (s_h2, H2_CR),
                         (s_add, ADD_CR), (s_idx, ROWS_CR), (s_ye, ROWS_CR),
                         (s_hid, HID_CR), (s_rTc, RTC_CR), (s_yps, YPS_CR)):
                dve.sem_inc(s, n)
            dve.memset(wcol[C:P, 0:1], 0.0).then_inc(s_dve, 1)
            dve.memset(eps[:, 0:1], EPS_GN).then_inc(s_dve, 1)
            dve.memset(eps[:, 1:2], EPS_LN).then_inc(s_dve, 1)
            dve.memset(eps[:, 2:3], 1.0).then_inc(s_dve, 1)
            dve.memset(dt.rearrange("p (d s) -> p d s", s=S)[:, :, 0:1], DT_RESTART).then_inc(s_dve, 1)
            dve.memset(bc[:, :, 0:1], 0.0).then_inc(s_dve, 1)
            ch.at = 6
            ch.link(dve.memset(xp1[:, :, C:C + 4], 1.0))
            dve.wait_ge(s_wcol, 16 * 5)
            dve.wait_ge(s_pool, 4)
            for m in range(3):
                dve.tensor_scalar(wconv[:, m, :], ident2[:, :], wcol[:, m:m + 1], None, ALU.mult
                                  ).then_inc(s_wconv, 1)
            dve.wait_ge(s_vecs, 16 * 6)
            with dve.Fori(0, CHUNKS) as c:
                for k in range(GPC):
                    g = GPC * c + k
                    dve.wait_ge(s_conv, g + 1)
                    y = hg[:, bass.ds(GL * g, GL), :]
                    dve.tensor_tensor(y, ps[:, 6 + [0, 1, 0][k], 0:GL * C].rearrange("p (l d) -> p l d", d=C),
                                      vecs[:, 0:1, :].broadcast_to([P, GL, C]), ALU.add).then_inc(s_y, 1)
                    dve.wait_ge(s_y, g + 1)
                    dve.bn_stats(stats[:, bass.ds(g, 1), :].rearrange("p a s -> p (a s)"),
                                 y.rearrange("p l d -> p (l d)")).then_inc(s_dve, 1)
            ch.at = 7 + NG
            dve.wait_ge(s_dve, ch.at)
            dve.bn_aggr(gn[:, 0:2], stats[:, :, :].rearrange("p g s -> p (g s)")).then_inc(s_gnvar, 1)
            dve.wait_ge(s_gnsd, 1)
            ch.link(dve.reciprocal(gn[:, 3:4], gn[:, 2:3]))
            def b_of(i):
                return vecs[:, i:i + 1, :].broadcast_to([P, CL, C])

            def group_norm(c):
                h = hg[:, CL * c:CL * (c + 1), :]
                ch.link(dve.scalar_tensor_tensor(out=h, in0=h, scalar=gn[:, 0:1], in1=b_of(1),
                                                 op0=ALU.subtract, op1=ALU.mult))
                ch.link(dve.scalar_tensor_tensor(out=h, in0=h, scalar=gn[:, 3:4], in1=b_of(2),
                                                 op0=ALU.mult, op1=ALU.add))
                ch.link(dve.scalar_tensor_tensor(out=gtmp, in0=h, scalar=0.0, in1=b_of(3),
                                                 op0=ALU.min, op1=ALU.mult))
                ch.link(dve.scalar_tensor_tensor(out=h, in0=h, scalar=0.0, in1=gtmp,
                                                 op0=ALU.max, op1=ALU.add))

            def centre(n, c):
                if n > 0:
                    dve.wait_ge(s_cen, n)
                h = hg[:, CL * c:CL * (c + 1), :]
                ch.link(dve.tensor_reduce(ln_s[:, 0, :], h, AX_X, ALU.add))
                ch.link(dve.tensor_scalar(ln_s[:, 3, :], ln_s[:, 0, :], 1.0 / C, None, ALU.mult))
                dve.tensor_tensor(cen[:, n % 2], h, ln_s[:, 3, :].unsqueeze(2).broadcast_to([P, CL, C]), ALU.subtract
                                  ).then_inc(s_cen, 1)

            def normalise(n, c):
                dve.wait_ge(s_sq, n + 1)
                dve.tensor_reduce(ln_s[:, 1, :], sq, AX_X, ALU.add).then_inc(s_var, 1)
                dve.wait_ge(s_sd, n + 1)
                ch.link(dve.reciprocal(ln_s[:, 0, :], ln_s[:, 2, :]))
                dve.wait_ge(s_cen, n + 1)
                dve.tensor_tensor(xp1[:, CL * c:CL * (c + 1), 0:C], cen[:, n % 2],
                                  ln_s[:, 0, :].unsqueeze(2).broadcast_to([P, CL, C]), ALU.mult
                                  ).then_inc(s_ln, 1)
                dve.wait_ge(s_ln, n + 1)

            def proj_copies(c):
                for g in range(GPC * c, GPC * (c + 1)):
                    dve.wait_ge(s_proj, g + 1)
                    t = banks((2 * (g % GPC) + 6) % 8, 2)[:, 0:GL * P].rearrange("p (l n) -> p l n", n=P)
                    dve.tensor_copy(dt.rearrange("p (d s) -> p d s", s=S)[:, :, 1 + GL * g:1 + GL * (g + 1)],
                                    t[:, :, 0:C].rearrange("p l n -> p n l")).then_inc(s_dve, 1)
                    dve.tensor_copy(bc[:, :, 1 + GL * g:1 + GL * (g + 1)],
                                    t[:, :, C:NPROJ].rearrange("p l n -> p n l")).then_inc(s_projc, 1)
                    ch.at = ch.at + 1

            group_norm(0)
            for c in range(CHUNKS):
                centre(c, c)
                if c + 1 < CHUNKS:
                    group_norm(c + 1)
                normalise(c, c)
                if c > 0:
                    proj_copies(c - 1)
            proj_copies(CHUNKS - 1)
            dve.wait_ge(s_projc, NG)
            dve.wait_ge(s_acols, 1)
            dve.tensor_scalar(a_exp[:, 1, :], a_exp[:, 0, :], -1.0, None, ALU.mult).then_inc(s_acols, 1)
            dve.tensor_scalar(a_exp[:, 2, :], a_exp[:, 0, :], -0.5, None, ALU.mult).then_inc(s_acols, 1)
            dve.reciprocal(a_exp[:, 3, :], a_exp[:, 0, :]).then_inc(s_acols, 1)
            dve.wait_ge(s_acols, 4)
            dve.tensor_tensor(bc[:, 0:N, :], bc[:, 0:N, :], a_exp[:, 3, :].unsqueeze(2).broadcast_to([P, N, S]),
                              ALU.mult).then_inc(s_bdiv, 1)
            dve.wait_ge(s_us, CHUNKS)
            parts = [[v[:, c * U:(c + 1) * U] for v in (tmp, dt, up, us_lg)] for c in range(NDC)]
            for c, (t, d, r, u) in enumerate(parts):
                dve.wait_ge(s_lnp, c + 1)
                ch.link(dve.scalar_tensor_tensor(out=d, in0=d, scalar=0.0, in1=t, op0=ALU.max, op1=ALU.add))
                dve.tensor_scalar(d, d, DT_MIN, None, ALU.max).then_inc(s_dt, 1)
            dve.wait_ge(s_dt, NDC)
            for c, (t, d, r, u) in enumerate(parts):
                dve.wait_ge(s_r0, c + 1)
                ch.link(dve.tensor_tensor(t, d, r, ALU.mult))
                ch.link(dve.scalar_tensor_tensor(out=t, in0=t, scalar=-2.0, in1=r, op0=ALU.add, op1=ALU.mult))
                dve.tensor_tensor(r, t, u, ALU.mult).then_inc(s_up, 1)

            def times_tanh(i, k):
                wv = w_ring[:, k % 4, :]
                dve.wait_ge(s_w, i + 1)
                dve.wait_ge(s_th, i + 1)
                dve.tensor_tensor(wv, banks(6, 2), wv, ALU.mult).then_inc(s_g, 1)

            def times_c(c, k):
                dve.wait_ge(s_h, c * N + k + 1 + H_CR)
                dve.wait_ge(s_add, c * (N + 1) + k + ADD_CR)
                dve.tensor_tensor(hc_buf(k), h_buf(k), bc[:, N + k:N + k + 1, :].broadcast_to([P, DC, S]),
                                  ALU.mult).then_inc(s_hcv, 1)

            def ssm_chunk(c, last):
                for k in range(N):
                    i = c * N + k
                    wv = w_ring[:, k % 4, :]
                    dA = banks(2 + 2 * (k % 2), 2)
                    dve.wait_ge(s_dA, i + 1)
                    dve.wait_ge(s_g, i + 1 + G_CR)
                    dve.scalar_tensor_tensor(out=wv, in0=dA, scalar=1.0, in1=wv, op0=ALU.add, op1=ALU.mult
                                             ).then_inc(s_b, 1)
                    if k + 1 < N or not last:
                        times_tanh(i + 1, k + 1)
                    if k - 1 in DVE_HC:
                        times_c(c, k - 1)
                    if (k - 2) % N in DVE_HC:
                        dve.wait_ge(s_hcv, c * NV + dve_upto(k - 2) + HCV_CR)
                    else:
                        dve.wait_ge(s_hcp, c * NPL + pool_upto(k - 2) + HCP_CR)
                    dve.wait_ge(s_b, i + 1)
                    dve.tensor_tensor_scan(hh_ring[:, k % 2, :], dA, wv, 0.0, ALU.mult, ALU.add
                                           ).then_inc(s_h, 1)
                if N - 1 in DVE_HC:
                    times_c(c, N - 1)

            times_tanh(0, 0)
            with dve.Fori(0, NDC - 1) as c:
                ssm_chunk(c, False)
            ssm_chunk(NDC - 1, True)

            dve.wait_ge(s_h2, NDC + H2_CR)
            dve.wait_ge(s_consts, 5)
            dve.tensor_copy(iota_e[:, :], iota_e_i[:, :]).then_inc(s_dve, 1)
            ch.at = ch.at + 1
            ch.link(dve.tensor_scalar(small_i[:, 0:2], tile_no_i[:, :], 2, None, ALU.logical_shift_right))
            ch.link(dve.tensor_tensor(tile_no[:, :], tile_no_i[:, :], small_i[:, 0:2], ALU.subtract))

            def choose(c):
                ls = range(CL * c, CL * (c + 1))
                span = slice(CL * c, CL * (c + 1))
                for g in range(GPC * c, GPC * (c + 1)):
                    dve.wait_ge(s_lg, g + 1)
                    dve.tensor_copy(logits[:, GL * g:GL * (g + 1), :],
                                    ps[:, 6 + g % 2, 0:GL * E].rearrange("p (l n) -> p l n", n=E)
                                    ).then_inc(s_lgc, 1)
                dve.wait_ge(s_lgc, GPC * (c + 1))
                for l in ls:
                    dve.max(mx[:, l, :], logits[:, l, :]).then_inc(s_dve, 1)
                ch.at = ch.at + CL
                dve.wait_ge(s_dve, ch.at)
                for l in ls:
                    dve.max_index(mi[:, l, :], mx[:, l, :], logits[:, l, :]).then_inc(s_dve, 1)
                ch.at = ch.at + CL
                dve.tensor_tensor(top[:, 0, span], mx[:, span, 1], mx[:, span, 0], ALU.subtract
                                  ).then_inc(s_ediff, 1)
                dve.wait_ge(s_dve, ch.at)
                dve.tensor_copy(top[:, 2, span], mi[:, span, 0]).then_inc(s_dve, 1)
                ch.at = ch.at + 1
                ch.link(dve.tensor_copy(top[:, 3, span], mi[:, span, 1]))
                ie = iota_e[:, :].unsqueeze(2).broadcast_to([P, E, CL])
                for j, m in ((2, mask1), (3, mask2)):
                    dve.tensor_tensor(m[:, :, span], ie, top[:, j:j + 1, span].broadcast_to([P, E, CL]),
                                      ALU.is_equal).then_inc(s_dve, 1)
                ch.at = ch.at + 2

            centre(CHUNKS, 0)
            for c in range(CHUNKS):
                if c + 1 < CHUNKS:
                    centre(CHUNKS + c + 1, c + 1)
                normalise(CHUNKS + c, c)
            for c in range(CHUNKS):
                choose(c)
            dve.wait_ge(s_dve, ch.at)
            ch.link(dve.tensor_tensor_scan(rank, hh_flat[:, 0:E * L], xt[:, C * S:C * S + E * L], 0.0,
                                           ALU.add, ALU.add))
            upto, cnt = small[:, 0, :], small[:, 1, :]
            ch.link(dve.tensor_copy(upto, rank3[:, :, L - 1]))
            dve.tensor_copy(cnt[:, 0:1], upto[:, 0:1]).then_inc(s_cnt, 1)
            dve.tensor_tensor(cnt[:, 1:E], upto[:, 1:E], upto[:, 0:E - 1], ALU.subtract).then_inc(s_cnt, 1)
            dve.wait_ge(s_tot, 2)
            tiles, ends, before, base, zero = (small[:, i, :] for i in (3, 4, 5, 6, 9))
            dve.memset(zero, 0.0).then_inc(s_dve, 1)
            ch.at = ch.at + 1
            ch.link(dve.tensor_scalar(small_i[:, :], ps[:, 0, 0:E], float(P - 1), None, ALU.add))
            ch.link(dve.tensor_scalar(small_i[:, :], small_i[:, :], P.bit_length() - 1, None,
                                      ALU.logical_shift_right))
            ch.link(dve.tensor_copy(tiles, small_i[:, :]))
            ch.link(dve.tensor_tensor_scan(ends, tiles, zero, 0.0, ALU.add, ALU.add))
            for j in range(2):
                ch.link(dve.tensor_scalar(small[:, 7 + j, :], ends, tile_no[:, j:j + 1], None, ALU.is_le))
                dve.tensor_reduce(tile_e[:, j:j + 1], small[:, 7 + j, :], AX_X, ALU.add).then_inc(s_te, 1)
            ch.link(dve.tensor_tensor(before, ends, tiles, ALU.subtract))
            ch.link(dve.scalar_tensor_tensor(out=before, in0=before, scalar=float(P), in1=ps[:, 1, 0:E],
                                             op0=ALU.mult, op1=ALU.add))
            dve.tensor_scalar(base[:, 0:1], before[:, 0:1], -1.0, None, ALU.add).then_inc(s_dve, 1)
            ch.at = ch.at + 1
            ch.link(dve.scalar_tensor_tensor(out=base[:, 1:E], in0=before[:, 1:E], scalar=-1.0,
                                             in1=upto[:, 0:E - 1], op0=ALU.add, op1=ALU.subtract))
            dve.tensor_copy(xp1[:, :, C + 1:C + 2], slot_i[:, 0, :].unsqueeze(2)).then_inc(s_dve, 1)
            dve.tensor_copy(xp2[:, :, C + 1:C + 2], slot_i[:, 1, :].unsqueeze(2)).then_inc(s_dve, 1)
            dve.memset(xp2[:, :, C + 3:C + 4], 0.0).then_inc(s_dve, 1)
            ch.at = ch.at + 3
            dve.wait_ge(s_eexp, 1)
            ch.link(dve.tensor_scalar(top[:, 4, :], top[:, 1, :], 1.0, None, ALU.add))
            ch.link(dve.reciprocal(top[:, 5, :], top[:, 4, :]))
            dve.tensor_copy(xp1[:, :, C + 2:C + 3], top[:, 5, :].unsqueeze(2)).then_inc(s_gate, 1)
            dve.tensor_tensor(xp2[:, :, C + 2:C + 3], top[:, 1, :].unsqueeze(2), top[:, 5, :].unsqueeze(2),
                              ALU.mult).then_inc(s_gate, 1)
            for k, m in enumerate((mask1, mask2)):
                for c in range(CHUNKS):
                    span = slice(CL * c, CL * (c + 1))
                    if k == 0:
                        ch.link(dve.tensor_tensor(rank3[:, :, span], rank3[:, :, span],
                                                  base.unsqueeze(2).broadcast_to([P, E, CL]), ALU.add))
                    ch.link(dve.tensor_tensor(m[:, :, span], m[:, :, span], rank3[:, :, span], ALU.mult))
                    ch.link(dve.tensor_reduce(top[:, 6, span], m[:, :, span].rearrange("p e l -> p l e"), AX_X,
                                              ALU.add))
                    dve.tensor_copy(slot_i[:, k, span], top[:, 6, span]).then_inc(s_slot, 1)
                dve.wait_ge(s_slot, CHUNKS * (k + 1))
            dve.wait_ge(s_teT, 1)
            dve.tensor_scalar(te[:, :], ps[0:1, 2, 0:2 * P], float(E - 1), None, ALU.min).then_inc(s_tei, 1)

            def relu(g, k):
                dve.wait_ge(s_hid, g + 1 + HID_CR)
                dve.wait_ge(s_yps, g - 1 + YPS_CR)
                dve.tensor_scalar(hT_e[:, k, :], ps[:, 2 + k, 0:TPG * P], 0.0, None, ALU.max
                                  ).then_inc(s_relu, 1)

            def gated(g, k, slot, landed, scattered):
                dve.wait_ge(s_rows[slot], landed)
                if scattered is not None:
                    dve.wait_ge(s_sc[k], 16 * TPG * scattered)
                dve.tensor_copy(out_idx[:, k, :], rows_in[:, slot, :, C + 1]).then_inc(s_idx, 1)
                es = experts(ET.DVE, g)
                dve.wait_ge(s_yps, g + 1 + YPS_CR)
                for t in range(TPG):
                    dve.tensor_tensor(y_e[:, k, t, :], ps[:, 4 + k, t * C:(t + 1) * C],
                                      b2s[:, bass.ds(es[t] * C, C)], ALU.add).then_inc(s_yb, 1)
                dve.wait_ge(s_yb, TPG * (g + 1))
                dve.tensor_tensor(y_e[:, k], y_e[:, k],
                                  rows_in[:, slot, :, C + 2:C + 3].broadcast_to([P, TPG, C]), ALU.mult
                                  ).then_inc(s_ye, 1)

            dve.wait_ge(s_b2, 16)
            dve.wait_ge(s_tei, 1)
            relu(0, 0)
            for g in range(RING):
                relu(g + 1, (g + 1) % 2)
                gated(g, g % 2, g, 16, g // 2 or None)
            with dve.Fori(1, GROUPS // RING) as q:
                for k in range(RING):
                    relu(RING * q + k + 1, (k + 1) % 2)
                    gated(RING * q + k, k % 2, k, 16 * (q + 1), RING // 2 * q + k // 2)
            for g in range(GROUPS - GROUPS % RING, GROUPS):
                if g + 1 < GROUPS:
                    relu(g + 1, (g + 1) % 2)
                gated(g, g % 2, g % RING, 16 * (g // RING + 1), g // 2)

            for c in range(CHUNKS):
                h = hg[:, c * CL:(c + 1) * CL, :]
                dve.wait_ge(s_yl[c], 32)
                ch.link(dve.tensor_tensor(h, h, y1[:, c * CL:(c + 1) * CL, :], ALU.add))
                dve.tensor_tensor(h, h, y2[:, c * CL:(c + 1) * CL, :], ALU.add).then_inc(s_fin, 1)


_INS = ["x", "L0_tok_w", "L0_tok_b", "L0_tok_gamma", "L0_tok_beta", "L0_tok_alpha", "L0_attn_A_log",
        "L0_attn_D_param", "L0_attn_scale", "L0_attn_W_dt", "L0_attn_b_dt", "L0_attn_W_B", "L0_attn_b_B",
        "L0_attn_W_C", "L0_attn_b_C", "L0_ffn_Wr", "L0_ffn_br", "L0_ffn_W1", "L0_ffn_b1", "L0_ffn_W2",
        "L0_ffn_b2"]


def kernel(**inputs):
    import numpy as _np
    import concourse.bacc as _bacc
    from concourse import mybir as _mybir
    from concourse.bass_utils import run_bass_kernel_spmd as _run

    nc = _bacc.Bacc("TRN2", target_bir_lowering=False, num_devices=1)
    arrays, args = {}, []
    for name in _INS:
        a = _np.ascontiguousarray(inputs[name])
        arrays[f"in_{name}"] = a
        args.append(nc.dram_tensor(f"in_{name}", a.shape, _mybir.dt.from_np(a.dtype), kind="ExternalInput").ap())
    args.append(nc.dram_tensor("out_dram", (P, L, C), F32, kind="ExternalOutput").ap())
    build(nc, *args)
    r = _run(nc, [arrays], core_ids=[0])
    return r.results[0]["out_dram"]
```
